# Optimizing a Trainium2 kernel written in Bass

```python
import numpy as np
import jax
import jax.numpy as jnp

def _softmax(x, axis=-1):
    return jax.nn.softmax(x, axis=axis)

def _gelu(x):
    return jax.nn.gelu(x, approximate=True)

def _silu(x):
    return jax.nn.silu(x)

def _sigmoid(x):
    return jax.nn.sigmoid(x)

def _layernorm(x, axis=-1, eps=1e-05):
    m = jnp.mean(x, axis=axis, keepdims=True)
    v = jnp.var(x, axis=axis, keepdims=True)
    return (x - m) / jnp.sqrt(v + eps)

def _scatter_add(tgt, idx, src, axis=0):
    return tgt.at[idx].add(src)

def _segment_sum(src, seg, n):
    return jax.ops.segment_sum(src, seg, n)
kernel_name = 'mk_cond_resid_d4_seqx_r4_7bdc89'

def setup_inputs(seed: int=0):
    np.random.seed(seed)
    _w = jnp.asarray

    def _rec_inputs():
        import jax
        import jax.numpy as jnp
        _rk = jax.random.key(seed)
        x = -0.0003929 + 0.9999 * jax.random.normal(jax.random.fold_in(_rk, 1), (128, 64, 1024), jnp.float32)
        _lenS = 64 - jax.random.randint(jax.random.fold_in(_rk, 7), (128,), 0, max(1, 64 // 4) + 1, jnp.int32)
        _lenS2 = 64 - jax.random.randint(jax.random.fold_in(_rk, 8), (128,), 0, max(1, 64 // 4) + 1, jnp.int32)
        itok_B_8_3872 = jax.random.randint(jax.random.fold_in(_rk, 11), (128,), 8, 3873, jnp.int32)
        itok_B_3_7 = jax.random.randint(jax.random.fold_in(_rk, 12), (128,), 3, 8, jnp.int32)
        itok_B_4_50 = jax.random.randint(jax.random.fold_in(_rk, 13), (128,), 4, 51, jnp.int32)
        itok_B_0_31 = jax.random.randint(jax.random.fold_in(_rk, 14), (128,), 0, 32, jnp.int32)
        return (x, itok_B_8_3872, itok_B_3_7, itok_B_4_50, itok_B_0_31)
    x, itok_B_8_3872, itok_B_3_7, itok_B_4_50, itok_B_0_31 = _rec_inputs()

    def _L0_cond_setup():
        import math
        import jax, jax.numpy as jnp
        import numpy as np
        H, N, B, L = (64, 64, 16, 1024)
        DT_MIN, DT_MAX = (0.001, 0.1)

        def _get_kernel(log_dt, C, log_A_real, A_imag, length):
            Cc = C[..., 0] + 1j * C[..., 1]
            dt = jnp.exp(log_dt)
            A = -jnp.exp(log_A_real) + 1j * A_imag
            dtA = A * dt[:, None]
            P = dtA[:, :, None] * jnp.arange(length, dtype=jnp.float32)
            Cs = Cc * (jnp.exp(dtA) - 1.0) / A
            K = 2.0 * jnp.einsum('hn,hnl->hl', Cs, jnp.exp(P)).real
            return K
        key = jax.random.key(seed)
        ks = jax.random.split(key, 6)
        u = jax.random.normal(ks[0], (B, H, L), dtype=jnp.float32)
        length = jax.random.randint(ks[1], (B,), 0, L)
        log_dt = jax.random.uniform(ks[2], (H,), dtype=jnp.float32) * (math.log(DT_MAX) - math.log(DT_MIN)) + math.log(DT_MIN)
        C = jax.random.normal(ks[3], (H, N, 2), dtype=jnp.float32)
        log_A_real = jnp.log(0.5 * jnp.ones((H, N), dtype=jnp.float32))
        A_imag = math.pi * jnp.broadcast_to(jnp.arange(N, dtype=jnp.float32), (H, N))
        D = jax.random.normal(ks[4], (H,), dtype=jnp.float32)
        return {'u': u, 'length': length, 'log_dt': log_dt, 'C': C, 'log_A_real': log_A_real, 'A_imag': A_imag, 'D': D}
    _L0_cond_all = _L0_cond_setup()
    _L0_cond_in = {k: v for k, v in _L0_cond_all.items() if k in ('log_dt', 'C', 'log_A_real', 'A_imag', 'D')}
    del _L0_cond_all

    def _L1_cond_setup():
        import jax, jax.numpy as jnp
        import numpy as np
        RANK = 16
        ALPHA = 16.0
        SCALING = ALPHA / RANK
        N_ADAPTERS = 8
        IN_F = 1024
        OUT_F = 1024
        BATCH = 4
        SEQ = 512
        key = jax.random.key(seed)
        kx, ka, kb, ki = jax.random.split(key, 4)
        x = jax.random.normal(kx, (BATCH, SEQ, IN_F), dtype=jnp.float32)
        A = jax.random.normal(ka, (N_ADAPTERS, OUT_F, RANK), dtype=jnp.float32) * 0.02
        B = jax.random.normal(kb, (N_ADAPTERS, RANK, IN_F), dtype=jnp.float32) * 0.02
        adapter_ids = jax.random.randint(ki, (BATCH,), 0, N_ADAPTERS, dtype=jnp.int32)
        return {'x': x, 'A': A, 'B': B, 'adapter_ids': adapter_ids}
    _L1_cond_all = _L1_cond_setup()
    _L1_cond_in = {k: v for k, v in _L1_cond_all.items() if k in ('A', 'B')}
    del _L1_cond_all

    def _L2_cond_setup():
        import jax, jax.numpy as jnp
        import numpy as np
        RANK = 16
        ALPHA = 16.0
        SCALING = ALPHA / RANK
        key = jax.random.key(seed)
        k1, k2, k3, k4 = jax.random.split(key, 4)
        batch, n_tok, d_in, d_out, n_adapters, rank = (8, 512, 1024, 1024, 64, RANK)
        x = jax.random.normal(k1, (batch, n_tok, d_in), dtype=jnp.float32)
        A = jax.random.normal(k2, (n_adapters, d_out, rank), dtype=jnp.float32) * 0.02
        B = jax.random.normal(k3, (n_adapters, rank, d_in), dtype=jnp.float32)
        adapter_ids = jax.random.randint(k4, (batch,), 0, n_adapters, dtype=jnp.int32)
        return {'x': x, 'A': A, 'B': B, 'adapter_ids': adapter_ids}
    _L2_cond_all = _L2_cond_setup()
    _L2_cond_in = {k: v for k, v in _L2_cond_all.items() if k in ('A', 'B')}
    del _L2_cond_all

    def _L3_cond_setup():
        import jax, jax.numpy as jnp
        import numpy as np
        S, C, D = (32, 64, 64)
        B, T = (64, 1024)
        key = jax.random.key(seed)
        k_x, k_w, k_s = jax.random.split(key, 3)
        x = jax.random.normal(k_x, (B, C, T), dtype=jnp.float32)
        subjects = jax.random.randint(k_s, (B,), 0, S, dtype=jnp.int64)
        std = float(np.sqrt(2.0 / (C + D)))
        weights = jax.random.normal(k_w, (S, C, D), dtype=jnp.float32) * std * (1.0 / np.sqrt(C))
        biases = jnp.zeros((S, 1, D), dtype=jnp.float32)
        return {'x': x, 'subjects': subjects, 'weights': weights, 'biases': biases}
    _L3_cond_all = _L3_cond_setup()
    _L3_cond_in = {k: v for k, v in _L3_cond_all.items() if k in ('weights', 'biases')}
    del _L3_cond_all
    return {'x': x, 'itok_B_8_3872': itok_B_8_3872, 'itok_B_3_7': itok_B_3_7, 'itok_B_4_50': itok_B_4_50, 'itok_B_0_31': itok_B_0_31, 'L0_cond_log_dt': _L0_cond_in['log_dt'], 'L0_cond_C': _L0_cond_in['C'], 'L0_cond_log_A_real': _L0_cond_in['log_A_real'], 'L0_cond_A_imag': _L0_cond_in['A_imag'], 'L0_cond_D': _L0_cond_in['D'], 'L1_cond_A': _L1_cond_in['A'], 'L1_cond_B': _L1_cond_in['B'], 'L2_cond_A': _L2_cond_in['A'], 'L2_cond_B': _L2_cond_in['B'], 'L3_cond_weights': _L3_cond_in['weights'], 'L3_cond_biases': _L3_cond_in['biases']}

def reference(x, itok_B_8_3872, itok_B_3_7, itok_B_4_50, itok_B_0_31, L0_cond_log_dt, L0_cond_C, L0_cond_log_A_real, L0_cond_A_imag, L0_cond_D, L1_cond_A, L1_cond_B, L2_cond_A, L2_cond_B, L3_cond_weights, L3_cond_biases):
    import jax
    import jax.numpy as jnp

    def _L0_cond_ref(u, length, log_dt, C, log_A_real, A_imag, D):
        import math
        import jax, jax.numpy as jnp
        import numpy as np
        H, N, B, L = (64, 64, 16, 1024)
        DT_MIN, DT_MAX = (0.001, 0.1)

        def _get_kernel(log_dt, C, log_A_real, A_imag, length):
            Cc = C[..., 0] + 1j * C[..., 1]
            dt = jnp.exp(log_dt)
            A = -jnp.exp(log_A_real) + 1j * A_imag
            dtA = A * dt[:, None]
            P = dtA[:, :, None] * jnp.arange(length, dtype=jnp.float32)
            Cs = Cc * (jnp.exp(dtA) - 1.0) / A
            K = 2.0 * jnp.einsum('hn,hnl->hl', Cs, jnp.exp(P)).real
            return K
        Bq, Hq, Lq = u.shape
        mask = (jnp.arange(Lq) < length[:, None]).astype(u.dtype)
        u_m = u * mask[:, None, :]
        kernel = _get_kernel(log_dt, C, log_A_real, A_imag, Lq)
        n = 2 * Lq
        k_f = jnp.fft.rfft(kernel, n=n)
        u_f = jnp.fft.rfft(u_m, n=n)
        y = jnp.fft.irfft(u_f * k_f, n=n)[..., :Lq]
        y = y + u_m * D[:, None]
        return y * mask[:, None, :]

    def _L1_cond_ref(x, A, B, adapter_ids):
        import jax, jax.numpy as jnp
        import numpy as np
        RANK = 16
        ALPHA = 16.0
        SCALING = ALPHA / RANK
        N_ADAPTERS = 8
        IN_F = 1024
        OUT_F = 1024
        BATCH = 4
        SEQ = 512
        B_sel = B[adapter_ids]
        A_sel = A[adapter_ids]
        Bx = jnp.einsum('bni,bri->bnr', x, B_sel)
        out = jnp.einsum('bnr,bor->bno', Bx, A_sel)
        return out * SCALING

    def _L2_cond_ref(x, A, B, adapter_ids):
        import jax, jax.numpy as jnp
        import numpy as np
        RANK = 16
        ALPHA = 16.0
        SCALING = ALPHA / RANK
        B_req = B[adapter_ids]
        A_req = A[adapter_ids]
        Bx = jnp.einsum('bni,bri->bnr', x, B_req)
        out = jnp.einsum('bnr,bor->bno', Bx, A_req)
        return out * SCALING

    def _L3_cond_ref(x, subjects, weights, biases):
        import jax, jax.numpy as jnp
        import numpy as np
        S, C, D = (32, 64, 64)
        B, T = (64, 1024)
        w = weights[subjects]
        b = biases[subjects]
        out = jnp.einsum('bct,bcd->bdt', x, w)
        return out + jnp.transpose(b, (0, 2, 1))
    x = x + _L0_cond_ref(x, itok_B_8_3872, L0_cond_log_dt, L0_cond_C, L0_cond_log_A_real, L0_cond_A_imag, L0_cond_D)
    x = x + _L1_cond_ref(x, L1_cond_A, L1_cond_B, itok_B_3_7)
    x = x + _L2_cond_ref(x, L2_cond_A, L2_cond_B, itok_B_4_50)
    x = x + _L3_cond_ref(x, itok_B_0_31, L3_cond_weights, L3_cond_biases)
    return x

_drawn_inputs = setup_inputs


def setup_inputs(seed=0):
    import zlib

    import numpy as np

    out = dict(_drawn_inputs(seed))
    spreads = {'L0_cond_log_A_real': (-0.6931471824645996, 0.2), 'L3_cond_biases': (0.0, 0.401)}
    factors = {}
    for name, (base, spread) in spreads.items():
        noise = np.random.default_rng([zlib.crc32(name.encode()), seed]).standard_normal(out[name].shape)
        drawn = base * np.exp(spread * noise) if base else spread * noise
        out[name] = jnp.asarray(drawn.astype(out[name].dtype))
    for name, factor in factors.items():
        out[name] = (out[name] * factor).astype(out[name].dtype)
    return out
```

```python
from contextlib import ExitStack


import concourse.bass as bass
from concourse import mybir

F32 = mybir.dt.float32
F16 = mybir.dt.float16
I32 = mybir.dt.int32
U8 = mybir.dt.uint8
ALU = mybir.AluOpType
ACT = mybir.ActivationFunctionType

P = 128
B = 128
H = 64
L = 1024
J = L // P
N = 64
R = 16
N1, N2, NS = 8, 64, 32
Q = B // 2
G = 1 + N2 * R // P
TC = 32
KPAD = L + P
A_SCALE = 64.0
GROW = N1 * R * N2
U = 4

MAGIC = 12582912.0
LOG2E = 1.4426950408889634
LN2_HI, LN2_LO = 0.693359375, -2.12194440e-4
TURN = 6.2831853071795865
TWO_PI = 6.283185
PI_2 = 1.5707963267948966


class Storage:
    pass


def storage(nc, ctx):
    m = Storage()

    def sb(name, shape, dt):
        return ctx.enter_context(nc.sbuf_tensor(name, shape, dt))

    m.k_rows = nc.dram_tensor("k_rows", (H, 2, KPAD), F16).ap()
    m.x1_rows = nc.dram_tensor("x1_rows", (B, H, L), F32).ap()
    m.a_rows = nc.dram_tensor("a_rows", (2 * (N1 + N2) * R, L), F16).ap()
    m.g_rows = nc.dram_tensor("g_rows", (GROW + R, R), F32).ap()

    m.xt = sb("xt", [P, U, L], F32)
    m.toep = sb("toep", [P, U, 2, L], F16)
    m.xTh = sb("xTh", [P, 2, J, P], F16)
    m.xTl = sb("xTl", [P, 2, J, P], F16)
    m.bt = sb("bt", [P, N1 + N2, 2, J, R], F16)
    m.iwh = sb("iwh", [P, Q, P], F16)
    m.iwl = sb("iwl", [P, Q, P], F16)
    m.g_pairs = sb("g_pairs", [64, Q, 2, R], F32)
    m.own = sb("own", [P, 2, H], F32)
    m.own_g = sb("own_g", [64, 2, R], F32)
    m.mask = sb("mask", [P, L], U8)
    m.ident = sb("ident", [P, P], F32)
    m.eye2 = sb("eye2", [P, H], F32)
    m.x1h = sb("x1h", [P, U, L], F16)
    m.x1l = sb("x1l", [P, U, L], F16)
    m.x1T = sb("x1T", [P, 2, J, P], F16)
    m.bsel = sb("bsel", [P, 2, 4, 2, J, R], F16)
    m.asel = sb("asel", [P, U, L], F16)
    m.outt = sb("outt", [P, 2, L], F32)
    m.ids = sb("ids", [P, 4, B], I32)
    m.sel_ids = sb("sel_ids", [1, Q, 2, 2], I32)
    m.idx_a = sb("idx_a", [P, Q], I32)
    m.idx_g = sb("idx_g", [P, Q], I32)
    m.idx_w = sb("idx_w", [P, Q], I32)
    m.idx_now = sb("idx_now", [P, U, 2], I32)
    m.bias_t = sb("bias_t", [P, Q], F32)
    m.zh = sb("zh", [P, 64], F16)
    m.zl = sb("zl", [P, 64], F16)
    m.qt = sb("qt", [64, P], F32)
    m.mp = sb("mp", [64, 2, 2, 64], F32)
    m.qh = sb("qh", [P, 2, P], F16)
    m.ql = sb("ql", [64, 2, P], F16)
    m.wnow = sb("wnow", [P, 2, H], F32)
    m.wboth = sb("wboth", [P, 2, P], F32)
    m.gnow = sb("gnow", [64, 2, R], F32)
    m.ps = ctx.enter_context(nc.psum_tensor("ps", [P, 8, 512], F32))
    return m


def setup_stage(nc, m, x, lens, id1, id2, id3, log_dt, C, log_A_real, A_imag, D, A1, B1, A2, B2, W, bias):
    ps, ident = m.ps, m.ident
    V, S, PE = nc.vector, nc.scalar, nc.tensor
    with ExitStack() as ctx:
        def sb(name, shape, dt):
            return ctx.enter_context(nc.sbuf_tensor(name, shape, dt))

        def sem(name):
            return ctx.enter_context(nc.semaphore(name))

        logs = sb("logs", [H, 72], F32)
        aim = sb("aim", [H, N], F32)
        cri = sb("cri", [H, N, 2], F32)
        work = sb("work", [H, 17, 72], F32)
        pow2 = sb("pow2", [H, 72], I32)
        packed = sb("packed", [H, 4, P], F32)
        par = sb("par", [P, 4, H], F32)
        step = sb("step", [P, 2, TC], F32)
        k0add = sb("k0add", [P, 16], F32)
        khl = sb("khl", [P, 2, 512], F16)
        zeros = sb("zeros", [P, P], F16)
        biases = sb("biases", [NS, H], F32)
        onehot = sb("onehot", [NS, B], F32)
        idf = sb("idf", [P, 4, B], F32)
        lenc = sb("lenc", [P, 1], I32)
        lenf = sb("lenf", [P, 1], F32)
        coli = sb("coli", [P, 4], I32)
        colf = sb("colf", [P, 4], F32)
        cols = sb("cols", [P, 12], F32)
        tmp = sb("tmp", [P, 2, Q], F32)

        def halves(t):
            f = t.rearrange("p a b -> p (a b)").bitcast(F32)
            return f[:, 0:H * TC], f[:, H * TC:2 * H * TC]

        turns_v, turns_u = halves(m.iwh[:])
        decay_v, decay_u = halves(m.iwl[:])
        sin_u = m.x1h[:].rearrange("p a b -> p (a b)").bitcast(F32)
        cos_u = m.x1l[:].rearrange("p a b -> p (a b)").bitcast(F32)
        kf = m.outt[:, 0, 0:512]
        a1f = m.outt[:, 0, :]
        iota_t = m.outt[:, 1, :]
        g_out = m.outt[:, 1, :]
        iota_i = m.bsel[:].rearrange("p a b c d e -> p (a b c d e)").bitcast(I32)
        nat_b = m.bsel[:].rearrange("p a b c d e -> p (a b c d e)").bitcast(F32)
        nat_a = m.x1T[:].rearrange("p a b c -> p (a b c)").bitcast(F32)
        by_k = m.toep[:, 0, :, :].rearrange("p a b -> p (a b)").bitcast(F32)
        at = m.asel[:, 0:2, :]
        a1c = m.asel[:, 2:4, :].rearrange("p s (j n) -> p s j n", j=J)

        def over_h(t):
            return t.rearrange("p (h c) -> p h c", c=TC)

        def blocks(k):
            return ps[:, k:k + 2, :].rearrange("p s (j n) -> p (s j) n", n=P)

        def by_adapter(k):
            return blocks(k).rearrange("p j (a r) -> p a j r", r=R)

        params_loaded = sem("params_loaded")
        ids_loaded = sem("ids_loaded")
        bias_loaded = sem("bias_loaded")
        const_made = sem("const_made")
        k0_cleared = sem("k0_cleared")
        iota_made = sem("iota_made")
        dve_step = sem("dve_step")
        angle_ready = sem("angle_ready")
        sine_ready = sem("sine_ready")
        packed_ready = sem("packed_ready")
        packed_turned = sem("packed_turned")
        par_ready = sem("par_ready")
        products = sem("products")
        decays = sem("decays")
        turns_v_ready, turns_u_ready = sem("turns_v_ready"), sem("turns_u_ready")
        abs_u_ready = sem("abs_u_ready")
        trig_v, trig_s, trig_c = sem("trig_v"), sem("trig_s"), sem("trig_c")
        uv_ready = sem("uv_ready")
        k_done = sem("k_done")
        khl_ready = sem("khl_ready")
        k_stored = sem("k_stored")
        onehot_ready, bias_done = sem("onehot_ready"), sem("bias_done")
        b_loaded, a_loaded = sem("b_loaded"), sem("a_loaded")
        a_ordered = sem("a_ordered")
        held = sem("held")
        b_turned, a_turned = sem("b_turned"), sem("a_turned")
        b_high, b_low, a_high, a_low = sem("b_high"), sem("b_low"), sem("a_high"), sem("a_low")
        a_stored = sem("a_stored")
        a1_copied, a1_back, a1_high, a1_low = sem("a1_copied"), sem("a1_back"), sem("a1_high"), sem("a1_low")
        g_done, g_ready, g_stored = sem("g_done"), sem("g_ready"), sem("g_stored")

        a_view = nat_a.rearrange("p (a n) -> p a n", a=8)
        a1_src = A1.rearrange("a (p k) r -> p a (k r)", k=J)
        a2_src = A2.rearrange("a (p k) r -> p a (k r)", k=J)
        b1_src = B1.rearrange("a r t -> (a r) t")
        b2_src = B2.rearrange("a r t -> (a r) t")
        a_dst = m.a_rows.rearrange("(s n) t -> n s t", s=2)

        with nc.Block() as block:
            @block.sync
            def _(sp):
                sp.dma_start(logs[:, 0:64], log_A_real).then_inc(params_loaded, 16)
                sp.dma_start(logs[:, 64:65], log_dt.rearrange("(h o) -> h o", o=1)).then_inc(params_loaded, 16)
                sp.dma_start(aim[:], A_imag).then_inc(params_loaded, 16)
                sp.dma_start(cri[:], C).then_inc(params_loaded, 16)
                sp.wait_ge(k0_cleared, 1)
                sp.dma_start(k0add[TC - 1:P:TC, :], D.rearrange("(q j) -> q j", j=16)).then_inc(params_loaded, 16)
                sp.dma_start(lenc[:], lens.rearrange("(b o) -> b o", o=1)).then_inc(ids_loaded, 16)
                for n, v in enumerate((lens, id1, id2, id3)):
                    sp.dma_start(m.ids[:, n, :], v.rearrange("(o b) -> o b", o=1).broadcast_to([P, B])).then_inc(ids_loaded, 16)
                sp.dma_start(biases[:], bias.rearrange("s o d -> s (o d)")).then_inc(bias_loaded, 16)
                sp.dma_start(a_view, a1_src).then_inc(a_loaded, 16)
                sp.wait_ge(iota_made, 2)
                sp.dma_start(nat_b, b1_src).then_inc(b_loaded, 16)
                sp.wait_ge(const_made, 4)
                sp.dma_start(m.k_rows[:, :, L:].rearrange("h s z -> (h s) z"), zeros[:]).then_inc(k_stored, 16)
                sp.dma_start(m.g_rows[GROW:GROW + R, :], ident[0:R, 0:R]).then_inc(g_stored, 16)
                sp.wait_ge(khl_ready, 1)
                for q in range(4):
                    for part in range(2):
                        sp.dma_start(
                            m.k_rows[16 * q:16 * q + 16, part, 0:L].rearrange("h (a c) -> a h c", c=TC),
                            khl[32 * q:32 * q + 32, part, :].rearrange("a (h c) -> a h c", c=TC)).then_inc(k_stored, 16)
                sp.wait_ge(a_low, 1)
                sp.dma_start(a_dst[0:P, :, :], at).then_inc(a_stored, 16)
                with sp.Fori(1, G) as g:
                    sp.wait_ge(b_turned, g)
                    sp.dma_start(nat_b, b2_src[bass.ds((g - 1) * P, P), :]).then_inc(b_loaded, 16)
                    sp.wait_ge(a_ordered, g)
                    sp.dma_start(a_view, a2_src[:, bass.ds((g - 1) * 8, 8), :]).then_inc(a_loaded, 16)
                    sp.wait_ge(a_low, g + 1)
                    sp.dma_start(a_dst[bass.ds(g * P, P), :, :], at).then_inc(a_stored, 16)
                sp.wait_ge(g_ready, 2)
                sp.dma_start(m.g_rows[0:GROW, :].rearrange("(n a) r -> n (a r)", n=P), g_out).then_inc(g_stored, 16)
                sp.wait_ge(g_stored, 32)
                sp.wait_ge(a_stored, 16 * G)
                sp.wait_ge(k_stored, 16 * 9)

            @block.gpsimd
            def _(gp):
                gp.memset(k0add[:], 0.0).then_inc(k0_cleared, 1)
                gp.memset(ident[:], 0.0).then_inc(const_made, 1)
                gp.wait_ge(const_made, 1)
                gp.affine_select(out=ident[:], in_=ident[:], compare_op=ALU.not_equal, fill=1.0, base=0,
                                 pattern=[[-1, P]], channel_multiplier=1).then_inc(const_made, 1)
                gp.iota(iota_i, pattern=[[1, L]], base=0, channel_multiplier=0).then_inc(iota_made, 1)
                gp.wait_ge(iota_made, 1)
                gp.tensor_copy(iota_t, iota_i).then_inc(iota_made, 1)
                gp.iota(coli[:, 0:1], pattern=[[0, 1]], base=0, channel_multiplier=1).then_inc(const_made, 1)
                gp.memset(zeros[:], 0.0).then_inc(const_made, 1)
                gp.wait_ge(par_ready, 1)
                for dst, src, s in ((turns_v, 1, 0), (turns_u, 1, 1), (decay_v, 0, 0), (decay_u, 0, 1)):
                    gp.tensor_tensor(over_h(dst), par[:, src, :].unsqueeze(2).broadcast_to([P, H, TC]),
                                     step[:, s, :].unsqueeze(1).broadcast_to([P, H, TC]), ALU.mult).then_inc(products, 1)

                def order(g, first):
                    gp.wait_ge(a_loaded, 16 * g + 16)
                    if not first:
                        gp.wait_ge(a_turned, g)
                    gp.sem_inc(held, 1)
                    gp.tensor_copy(by_k.rearrange("p (k a r) -> p k a r", k=J, a=8),
                                   nat_a.rearrange("p (a k r) -> p k a r", a=8, k=J)).then_inc(a_ordered, 1)

                order(0, True)
                with gp.Fori(1, G) as g:
                    order(g, False)

            @block.scalar
            def _(act):
                act.wait_ge(angle_ready, 1)
                S.activation(work[:, 10, 0:64], work[:, 9, 0:64], ACT.Sin, scale=TWO_PI).then_inc(sine_ready, 1)
                S.activation(work[:, 11, 0:64], work[:, 9, 0:64], ACT.Sin, scale=TWO_PI / 2).then_inc(sine_ready, 1)
                act.wait_ge(products, 4)
                S.activation(decay_v, decay_v, ACT.Exp).then_inc(decays, 1)
                S.activation(decay_u, decay_u, ACT.Exp).then_inc(decays, 1)
                act.wait_ge(turns_v_ready, 1)
                S.activation(turns_v, turns_v, ACT.Sin, scale=cols[:, 0:1], bias=cols[:, 1:2]).then_inc(trig_v, 1)
                act.wait_ge(turns_u_ready, 1)
                S.activation(sin_u, turns_u, ACT.Sin, scale=TWO_PI).then_inc(trig_s, 1)
                act.wait_ge(abs_u_ready, 1)
                S.activation(cos_u, cos_u, ACT.Sin, scale=-TWO_PI, bias=cols[:, 2:3]).then_inc(trig_c, 1)

                def high_parts(g, dst, first):
                    act.wait_ge(b_turned, g + 1)
                    S.activation(dst, by_adapter(2), ACT.Copy).then_inc(b_high, 1)
                    act.wait_ge(a_turned, g + 1)
                    if not first:
                        act.wait_ge(a_stored, 16 * g)
                    S.activation(at[:, 0, :].rearrange("p (t k) -> p t k", k=J),
                                 blocks(4).rearrange("p k t -> p t k"), ACT.Copy, scale=A_SCALE).then_inc(a_high, 1)

                high_parts(0, m.bt[:, 0:N1, 0, :, :], True)
                act.wait_ge(a1_back, 1)
                S.activation(a1c[:, 0, :, :], blocks(6), ACT.Copy, scale=A_SCALE).then_inc(a1_high, 1)
                with act.Fori(1, G) as g:
                    high_parts(g, m.bt[:, bass.ds(g * 8, 8), 0, :, :], False)
                act.wait_ge(g_done, 1)
                for n in range(2):
                    S.activation(g_out[:, n * 512:(n + 1) * 512], ps[:, 6 + n, :], ACT.Copy, scale=1 / A_SCALE).then_inc(g_ready, 1)

            @block.tensor
            def _(pe):
                pe.wait_ge(const_made, 2)
                pe.wait_ge(packed_ready, 1)
                for n in range(4):
                    last = PE.transpose(ps[:, 1, n * H:(n + 1) * H], packed[:, n, :], ident[0:H, 0:H])
                last.then_inc(packed_turned, 1)
                pe.wait_ge(uv_ready, 1)
                for h in range(H):
                    q, j = h // 16, h % 16
                    last = PE.matmul(ps[32 * q:32 * q + 32, 0, j * TC:(j + 1) * TC], over_h(cos_u)[:, h, :],
                                     over_h(turns_v)[:, h, :], start=True, stop=True)
                last.then_inc(k_done, 1)
                pe.wait_ge(bias_loaded, 16)
                pe.wait_ge(onehot_ready, 1)
                for b in range(2):
                    last = PE.matmul(ps[64 * b:64 * b + 64, 1, 256:256 + Q], biases[:],
                                     onehot[:].rearrange("s (q b) -> s b q", b=2)[:, b, :], start=True, stop=True)
                last.then_inc(bias_done, 1)

                def turn_group(g, first):
                    pe.wait_ge(b_loaded, 16 * g + 16)
                    if not first:
                        pe.wait_ge(b_low, g)
                    for j in range(J):
                        last = PE.transpose(blocks(2)[:, j, :], nat_b[:, j * P:(j + 1) * P], ident[:])
                    last.then_inc(b_turned, 1)
                    pe.wait_ge(a_ordered, g + 1)
                    if not first:
                        pe.wait_ge(a_low, g)
                    for k in range(J):
                        last = PE.transpose(blocks(4)[:, k, :], by_k[:, k * P:(k + 1) * P], ident[:])
                    last.then_inc(a_turned, 1)

                turn_group(0, True)
                pe.wait_ge(a1_copied, 1)
                for j in range(J):
                    last = PE.transpose(blocks(6)[:, j, :], a1f[:, j * P:(j + 1) * P], ident[:])
                last.then_inc(a1_back, 1)
                with pe.Fori(1, G) as g:
                    turn_group(g, False)
                pe.wait_ge(a1_low, 1)
                pe.wait_ge(b_low, G)
                for n in range(2):
                    for j in range(J):
                        for k, (a, b) in enumerate(((0, 0), (0, 1), (1, 0))):
                            last = PE.matmul(ps[:, 6 + n, :], a1c[:, a, j, :], m.bt[:, N1 + n * 32:N1 + (n + 1) * 32, b, j, :],
                                             start=(j == 0 and k == 0), stop=(j == J - 1 and k == 2))
                last.then_inc(g_done, 1)

            @block.vector
            def _(dve):
                steps = [0]

                def link(ins):
                    steps[0] += 1
                    ins.then_inc(dve_step, 1)
                    dve.wait_ge(dve_step, steps[0])

                def t(n, w=64):
                    return work[:, n, 0:w]

                def exp_parts(src, w):
                    k, r, e = t(0, w), t(1, w), t(2, w)
                    link(V.tensor_scalar(k, src, LOG2E, MAGIC, ALU.mult, ALU.add))
                    link(V.tensor_scalar(k, k, MAGIC, -126.0, ALU.subtract, ALU.max))
                    link(V.scalar_tensor_tensor(r, k, -LN2_HI, src, ALU.mult, ALU.add))
                    link(V.scalar_tensor_tensor(r, k, -LN2_LO, r, ALU.mult, ALU.add))
                    link(V.tensor_scalar(e, r, 1 / 5040, None, ALU.mult))
                    for c in (1 / 720, 1 / 120, 1 / 24, 1 / 6, 1 / 2, 1.0):
                        link(V.scalar_tensor_tensor(e, e, c, r, ALU.add, ALU.mult))
                    link(V.tensor_scalar(pow2[:, 0:w], k, 127.0, 8388608.0, ALU.add, ALU.mult))
                    link(V.tensor_copy(t(3, w), pow2[:, 0:w].bitcast(F32)))

                dve.wait_ge(params_loaded, 80)
                exp_parts(logs[:, 0:65], 65)
                link(V.scalar_tensor_tensor(t(4, 65), t(2, 65), 1.0, t(3, 65), ALU.add, ALU.mult))
                nar, dt = t(4), work[:, 4, 64:65]
                link(V.tensor_scalar(t(5), nar, dt, -1.0, ALU.mult, ALU.mult))
                link(V.tensor_scalar(t(6), aim[:], dt, 1 / TURN, ALU.mult, ALU.mult))
                link(V.tensor_scalar(t(7), t(6), MAGIC, None, ALU.add))
                link(V.tensor_scalar(t(8), t(7), MAGIC, None, ALU.subtract))
                V.tensor_tensor(t(9), t(6), t(8), ALU.subtract).then_inc(angle_ready, 1)
                exp_parts(t(5), 64)
                link(V.tensor_tensor(t(0), t(2), t(3), ALU.mult))
                link(V.scalar_tensor_tensor(t(1), t(3), -1.0, t(0), ALU.add, ALU.add))
                link(V.tensor_scalar(t(2), t(1), 1.0, None, ALU.add))
                dve.wait_ge(sine_ready, 2)
                link(V.tensor_tensor(t(7), t(2), t(10), ALU.mult))
                link(V.tensor_tensor(t(8), t(11), t(11), ALU.mult))
                link(V.tensor_tensor(t(8), t(8), t(2), ALU.mult))
                link(V.scalar_tensor_tensor(t(12), t(8), -2.0, t(1), ALU.mult, ALU.add))
                link(V.tensor_tensor(t(0), nar, nar, ALU.mult))
                link(V.tensor_tensor(t(1), aim[:], aim[:], ALU.mult))
                link(V.tensor_tensor(t(0), t(0), t(1), ALU.add))
                link(V.reciprocal(t(0), t(0)))
                link(V.tensor_tensor(t(2), t(12), nar, ALU.mult))
                link(V.tensor_tensor(t(3), t(7), aim[:], ALU.mult))
                link(V.tensor_tensor(t(2), t(3), t(2), ALU.subtract))
                link(V.tensor_tensor(t(13), t(2), t(0), ALU.mult))
                link(V.tensor_tensor(t(2), t(7), nar, ALU.mult))
                link(V.tensor_tensor(t(3), t(12), aim[:], ALU.mult))
                link(V.tensor_tensor(t(2), t(2), t(3), ALU.add))
                link(V.scalar_tensor_tensor(t(14), t(2), -1.0, t(0), ALU.mult, ALU.mult))
                cr, ci = cri[:, :, 0], cri[:, :, 1]
                link(V.tensor_tensor(t(0), cr, t(13), ALU.mult))
                link(V.tensor_tensor(t(1), ci, t(14), ALU.mult))
                link(V.tensor_tensor(t(15), t(0), t(1), ALU.subtract))
                link(V.tensor_tensor(t(0), cr, t(14), ALU.mult))
                link(V.tensor_tensor(t(1), ci, t(13), ALU.mult))
                link(V.tensor_tensor(t(16), t(0), t(1), ALU.add))
                for half in (slice(0, 64), slice(64, 128)):
                    link(V.tensor_copy(packed[:, 0, half], t(5)))
                    link(V.tensor_copy(packed[:, 1, half], t(6)))
                link(V.tensor_scalar(packed[:, 2, 0:64], t(15), 2.0, None, ALU.mult))
                link(V.tensor_scalar(packed[:, 2, 64:128], t(16), -2.0, None, ALU.mult))
                link(V.tensor_scalar(packed[:, 3, 0:64], t(16), 2.0, None, ALU.mult))
                link(V.tensor_scalar(packed[:, 3, 64:128], t(15), 2.0, None, ALU.mult))
                dve.wait_ge(iota_made, 2)
                link(V.tensor_scalar(step[:, 0, :], iota_t[:, 0:TC], -1.0, TC - 1.0, ALU.mult, ALU.add))
                link(V.tensor_scalar(step[:, 1, :], step[:, 0, :], float(TC), None, ALU.mult))
                link(V.memset(cols[0:64, 0:1], -TWO_PI))
                link(V.memset(cols[64:128, 0:1], TWO_PI))
                link(V.memset(cols[0:64, 1:2], PI_2))
                link(V.memset(cols[64:128, 1:2], 0.0))
                V.memset(cols[:, 2:3], PI_2).then_inc(packed_ready, 1)
                dve.wait_ge(packed_turned, 1)
                V.tensor_copy(par[:], ps[:, 1, 0:4 * H].rearrange("p (n h) -> p n h", n=4)).then_inc(par_ready, 1)

                dve.wait_ge(ids_loaded, 80)
                dve.wait_ge(const_made, 3)
                link(V.tensor_copy(idf[:], m.ids[:]))
                link(V.tensor_copy(lenf[:], lenc[:]))
                link(V.tensor_scalar(m.mask[:], iota_t, lenf[:, 0:1], None, ALU.is_lt))
                link(V.tensor_scalar(coli[:, 1:2], coli[:, 0:1], 4, 1, ALU.logical_shift_right, ALU.bitwise_and))
                link(V.tensor_scalar(coli[:, 2:3], coli[:, 0:1], 15, None, ALU.bitwise_and))
                link(V.tensor_scalar(coli[:, 3:4], coli[:, 0:1], 6, None, ALU.logical_shift_right))
                link(V.tensor_copy(colf[:], coli[:]))
                pf, lf, rf, sf = (colf[:, n:n + 1] for n in range(4))

                def col(n, rows=slice(0, P)):
                    return cols[rows, n:n + 1]

                link(V.tensor_scalar(col(3), lf, -1.0, 1.0, ALU.mult, ALU.add))
                link(V.tensor_scalar(col(4), col(3), float(R), None, ALU.mult))
                link(V.tensor_scalar(col(5), lf, float(R), None, ALU.mult))
                link(V.scalar_tensor_tensor(col(6), sf, float((N1 + N2) * R), rf, ALU.mult, ALU.add))
                link(V.scalar_tensor_tensor(col(6), lf, float(N1 * R), col(6), ALU.mult, ALU.add))
                link(V.tensor_scalar(col(7), col(3), float(R * N2), None, ALU.mult))
                link(V.scalar_tensor_tensor(col(8), col(3), float(N2), lf, ALU.mult, ALU.add))
                link(V.tensor_tensor(col(8), col(8), rf, ALU.mult))
                link(V.scalar_tensor_tensor(col(8), lf, float(GROW), col(8), ALU.mult, ALU.add))
                link(V.scalar_tensor_tensor(col(9), sf, -64.0, pf, ALU.mult, ALU.add))
                pair = idf[:].rearrange("p n (q b) -> p n b q", b=2)
                for k in range(4):
                    rows, b = slice(32 * k, 32 * k + 32), k % 2
                    link(V.tensor_scalar(tmp[rows, 0, :], pair[rows, 1, b, :], col(4, rows), col(6, rows), ALU.mult, ALU.add))
                    link(V.scalar_tensor_tensor(m.idx_a[rows, :], pair[rows, 2, b, :], col(5, rows), tmp[rows, 0, :], ALU.mult, ALU.add))
                    link(V.tensor_scalar(tmp[rows, 1, :], pair[rows, 1, b, :], col(7, rows), col(8, rows), ALU.mult, ALU.add))
                    link(V.scalar_tensor_tensor(m.idx_g[rows, :], pair[rows, 2, b, :], col(3, rows), tmp[rows, 1, :], ALU.mult, ALU.add))
                for b in range(2):
                    rows = slice(64 * b, 64 * b + 64)
                    link(V.tensor_scalar(m.idx_w[rows, :], pair[rows, 3, b, :], float(H), col(9, rows), ALU.mult, ALU.add))
                    link(V.tensor_copy(m.eye2[rows, :], ident[rows, 64 * b:64 * b + 64]))
                for layer in range(2):
                    link(V.tensor_copy(m.sel_ids[:, :, :, layer], m.ids[0:1, 1 + layer, :].rearrange("o (q b) -> o q b", b=2)))
                V.tensor_scalar(onehot[:], idf[0:NS, 3, :], pf[0:NS, :], None, ALU.is_equal).then_inc(onehot_ready, 1)
                link(V.memset(m.own[:], 0.0))
                link(V.memset(m.own_g[:], 0.0))
                for b in range(2):
                    link(V.memset(m.own[64 * b:64 * b + 64, b, :], 1.0))
                    link(V.memset(m.own_g[32 * b:32 * b + 32, b, :], 1.0))
                link(V.tensor_scalar(coli[:, 1:2], coli[:, 0:1], TC - 1, None, ALU.bitwise_and))
                link(V.tensor_copy(col(10), coli[:, 1:2]))
                link(V.tensor_scalar(col(10), col(10), TC - 1.0, None, ALU.is_equal))
                link(V.tensor_scalar(k0add[:], k0add[:], col(10), None, ALU.add))

                dve.wait_ge(products, 2)
                link(V.tensor_scalar(sin_u, turns_v, MAGIC, MAGIC, ALU.add, ALU.subtract))
                link(V.tensor_tensor(turns_v, turns_v, sin_u, ALU.subtract))
                V.scalar_tensor_tensor(turns_v[0:64, :], turns_v[0:64, :], -1.0, turns_v[0:64, :], ALU.mult, ALU.max).then_inc(turns_v_ready, 1)
                link(V.tensor_scalar(cos_u, turns_u, MAGIC, MAGIC, ALU.add, ALU.subtract))
                V.tensor_tensor(turns_u, turns_u, cos_u, ALU.subtract).then_inc(turns_u_ready, 1)
                dve.wait_ge(turns_u_ready, 1)
                V.scalar_tensor_tensor(cos_u, turns_u, -1.0, turns_u, ALU.mult, ALU.max).then_inc(abs_u_ready, 1)
                dve.wait_ge(trig_v, 1)
                dve.wait_ge(decays, 2)
                link(V.tensor_tensor(turns_v, turns_v, decay_v, ALU.mult))
                dve.wait_ge(trig_s, 1)
                link(V.tensor_tensor(over_h(sin_u), over_h(sin_u), par[:, 3, :].unsqueeze(2).broadcast_to([P, H, TC]), ALU.mult))
                dve.wait_ge(trig_c, 1)
                link(V.tensor_tensor(over_h(cos_u), over_h(cos_u), par[:, 2, :].unsqueeze(2).broadcast_to([P, H, TC]), ALU.mult))
                link(V.tensor_tensor(cos_u, cos_u, sin_u, ALU.subtract))
                V.tensor_tensor(cos_u, cos_u, decay_u, ALU.mult).then_inc(uv_ready, 1)
                dve.wait_ge(k_done, 1)
                link(V.tensor_copy(kf, ps[:, 0, :]))
                k0 = over_h(kf)[:, :, TC - 1]
                link(V.tensor_tensor(k0, k0, k0add[:], ALU.add))
                link(V.tensor_copy(khl[:, 0, :], kf))
                V.tensor_tensor(khl[:, 1, :], kf, khl[:, 0, :], ALU.subtract).then_inc(khl_ready, 1)
                dve.wait_ge(khl_ready, 1)
                dve.wait_ge(bias_done, 1)
                link(V.tensor_copy(m.bias_t[:], ps[:, 1, 256:256 + Q]))

                def low_parts(g, high, low, first):
                    dve.wait_ge(b_high, g + 1)
                    V.tensor_tensor(low, by_adapter(2), high, ALU.subtract).then_inc(b_low, 1)
                    dve.wait_ge(a_high, g + 1)
                    turned = blocks(4).rearrange("p k t -> p t k")
                    if first:
                        V.tensor_copy(a1f.rearrange("p (t k) -> p t k", k=J), turned).then_inc(a1_copied, 1)
                    V.scalar_tensor_tensor(at[:, 1, :].rearrange("p (t k) -> p t k", k=J), turned, A_SCALE,
                                           at[:, 0, :].rearrange("p (t k) -> p t k", k=J), ALU.mult, ALU.subtract).then_inc(a_low, 1)

                low_parts(0, m.bt[:, 0:N1, 0, :, :], m.bt[:, 0:N1, 1, :, :], True)
                dve.wait_ge(a1_high, 1)
                V.scalar_tensor_tensor(a1c[:, 1, :, :], blocks(6), A_SCALE, a1c[:, 0, :, :], ALU.mult, ALU.subtract).then_inc(a1_low, 1)
                with dve.Fori(1, G) as g:
                    group = bass.ds(g * 8, 8)
                    low_parts(g, m.bt[:, group, 0, :, :], m.bt[:, group, 1, :, :], False)


def channel_stage(nc, m, x, W):
    ps, ident = m.ps, m.ident
    V, S, PE, GP = nc.vector, nc.scalar, nc.tensor, nc.gpsimd
    TURNS = H // U
    with ExitStack() as ctx:
        def sem(name):
            return ctx.enter_context(nc.semaphore(name))

        x_loaded = [sem(f"x_loaded{u}") for u in range(U)]
        toep_loaded = [sem(f"toep_loaded{u}") for u in range(U)]
        x1_stored = [sem(f"x1_stored{u}") for u in range(U)]
        xT_done = sem("xT_done")
        xTh_ready = sem("xTh_ready")
        xTl_ready = sem("xTl_ready")
        conv_done = sem("conv_done")
        x1_ready = sem("x1_ready")
        idx_copied = sem("idx_copied")
        held = sem("held")
        held_gather = sem("held_gather")
        w_gathered = [sem(f"w_gathered{u}") for u in range(2)]
        g_gathered = [sem(f"g_gathered{u}") for u in range(2)]
        w_both = sem("w_both")
        w_plus = sem("w_plus")
        w_high = sem("w_high")
        w_low = sem("w_low")
        g_kept = sem("g_kept")

        def turned(h2):
            return ps[:, 2 * h2:2 * h2 + 2, :].rearrange("p s (j n) -> p (s j) n", n=P)

        def conv_out(h2):
            return ps[:, 4 + 2 * h2:6 + 2 * h2, :]

        def turns(eng, body):
            body(0, True, False)
            with eng.Fori(1, TURNS - 1) as i:
                body(i, False, False)
            body(TURNS - 1, False, True)

        with nc.Block() as block:
            @block.sync
            def _(sp):
                def load(h, u):
                    sp.dma_start(m.xt[:, u, :], x[:, bass.ds(h, 1), :].rearrange("b o t -> b (o t)")).then_inc(x_loaded[u], 16)
                    row = bass.AP(m.k_rows.tensor, h * (2 * KPAD), [[1, P], [KPAD, 2], [1, L]])
                    sp.dma_start(m.toep[:, u, :, :], row).then_inc(toep_loaded[u], 16)

                def body(i, first, last):
                    for u in range(U):
                        h = i * U + u
                        sp.wait_ge(x1_ready, h + 1)
                        sp.dma_start(m.x1_rows[:, bass.ds(h, 1), :].rearrange("b o t -> b (o t)"), m.xt[:, u, :]).then_inc(x1_stored[u], 16)
                        if last and u:
                            continue
                        v = (u + 3) % U
                        if not (first and u == 0):
                            sp.wait_ge(x1_stored[v], 16 * (i + (1 if u else 0)))
                        load(h + 3, v)

                for h in range(3):
                    load(h, h)
                turns(sp, body)
                for u in range(U):
                    sp.wait_ge(x1_stored[u], 16 * TURNS)

            @block.gpsimd
            def _(gp):
                w_src = W.rearrange("s c d -> (s c) d")

                def body(i, first, last):
                    for u in range(U):
                        q, v = i * U + u, u % 2
                        GP.tensor_copy(m.idx_now[:, v, 0:1], m.idx_w[:, bass.ds(q, 1)]).then_inc(idx_copied, 1)
                        GP.tensor_copy(m.idx_now[:, v, 1:2], m.idx_g[:, bass.ds(q, 1)]).then_inc(idx_copied, 1)
                        gp.wait_ge(idx_copied, 2 * q + 2)
                        gp.sem_inc(held_gather, 1)
                        gp.indirect_dma_start(m.wnow[:, v, :], None, w_src,
                                              bass.IndirectOffsetOnAxis(ap=m.idx_now[:, v, 0:1], axis=0)).then_inc(w_gathered[v], 16)
                        gp.indirect_dma_start(m.gnow[:, v, :], None, m.g_rows,
                                              bass.IndirectOffsetOnAxis(ap=m.idx_now[0:64, v, 1:2], axis=0)).then_inc(g_gathered[v], 16)
                        gp.wait_ge(w_gathered[v], 16 * (2 * i + u // 2 + 1))
                        GP.tensor_tensor(m.wnow[:, v, :], m.wnow[:, v, :], m.eye2[:], ALU.add).then_inc(w_plus, 1)
                        gp.wait_ge(g_gathered[v], 16 * (2 * i + u // 2 + 1))
                        GP.tensor_tensor(m.g_pairs[:, bass.ds(q, 1), :, :].rearrange("p o b r -> p (o b) r"),
                                         m.gnow[:, v:v + 1, :].broadcast_to([64, 2, R]), m.own_g[:], ALU.mult).then_inc(g_kept, 1)
                        gp.wait_ge(w_plus, q + 1)
                        both = m.wboth[:, v, :]
                        GP.tensor_tensor(both.rearrange("p (b d) -> p b d", b=2), m.wnow[:, v:v + 1, :].broadcast_to([P, 2, H]),
                                         m.own[:], ALU.mult).then_inc(w_both, 1)
                        gp.wait_ge(w_both, q + 1)
                        high = m.iwh[:, bass.ds(q, 1), :].rearrange("p o d -> p (o d)")
                        GP.tensor_copy(high, both).then_inc(w_high, 1)
                        gp.wait_ge(w_high, q + 1)
                        GP.tensor_tensor(m.iwl[:, bass.ds(q, 1), :].rearrange("p o d -> p (o d)"), both, high,
                                         ALU.subtract).then_inc(w_low, 1)

                turns(gp, body)
                gp.wait_ge(w_low, Q)

            @block.scalar
            def _(act):
                def body(i, first, last):
                    for u in range(U):
                        h = i * U + u
                        act.wait_ge(xT_done, h + 1)
                        if not (first and u < 2):
                            act.wait_ge(conv_done, h - 1)
                        S.activation(m.xTh[:, u % 2, :, :], turned(u % 2), ACT.Copy).then_inc(xTh_ready, 1)

                turns(act, body)

            @block.vector
            def _(dve):
                def low_part(h, u):
                    dve.wait_ge(xTh_ready, h + 1)
                    V.tensor_tensor(m.xTl[:, u % 2, :, :], turned(u % 2), m.xTh[:, u % 2, :, :], ALU.subtract).then_inc(xTl_ready, 1)

                def body(i, first, last):
                    for u in range(U):
                        h = i * U + u
                        if not (last and u == 3):
                            low_part(h + 1, u + 1)
                        dve.wait_ge(conv_done, h + 1)
                        dve.sem_inc(held, 1)
                        V.copy_predicated(m.xt[:, u, :], m.mask[:], conv_out(u % 2).rearrange("p s n -> p (s n)")[:, ::-1]).then_inc(x1_ready, 1)

                low_part(0, 0)
                turns(dve, body)

            @block.tensor
            def _(pe):
                def turn(i, u, early):
                    h = i * U + u
                    pe.wait_ge(x_loaded[u % U], 16 * (i + 1 + u // U))
                    if not early:
                        pe.wait_ge(xTl_ready, h - 1)
                    for j in range(J):
                        last = PE.transpose(turned(u % 2)[:, j, :], m.xt[:, u % U, j * P:(j + 1) * P], ident[:])
                    last.then_inc(xT_done, 1)

                def convolve(i, u, early):
                    h = i * U + u
                    out = conv_out(u % 2)
                    pe.wait_ge(xTl_ready, h + 1)
                    pe.wait_ge(toep_loaded[u], 16 * (i + 1))
                    if not early:
                        pe.wait_ge(x1_ready, h - 1)
                    for j in range(J):
                        for k, (xT, part) in enumerate(((m.xTh, 0), (m.xTh, 1), (m.xTl, 0))):
                            for bank in range(2 if j < 4 else 1):
                                y0, y1 = bank * 512, min(bank * 512 + 512, L - j * P)
                                last = PE.matmul(out[:, bank, 0:y1 - y0], xT[:, u % 2, j, :],
                                                 m.toep[:, u, part, y0 + j * P:y1 + j * P],
                                                 start=(j == 0 and k == 0), stop=(j == 7 - 4 * bank and k == 2))
                    last.then_inc(conv_done, 1)

                def body(i, first, last):
                    for u in range(U):
                        if not (last and u == 3):
                            turn(i, u + 1, first and u + 1 < 2)
                        convolve(i, u, first and u < 2)

                turn(0, 0, True)
                turns(pe, body)


def pair_stage(nc, m, out):
    ps, ident = m.ps, m.ident
    V, S, PE, GP = nc.vector, nc.scalar, nc.tensor, nc.gpsimd
    TURNS = Q // U
    with ExitStack() as ctx:
        def sem(name):
            return ctx.enter_context(nc.semaphore(name))

        x1_loaded = [sem(f"x1_loaded{u}") for u in range(U)]
        a_gathered = [sem(f"a_gathered{u}") for u in range(U)]
        out_stored = [sem(f"out_stored{u}") for u in range(2)]
        cleared = sem("cleared")
        a_idx = sem("a_idx")
        held_gather = sem("held_gather")
        b_selected = sem("b_selected")
        m_selected = sem("m_selected")
        turned_done, z_done, qt_done, mq_done, o_done = (sem(n) for n in ("turned_done", "z_done", "qt_done", "mq_done", "o_done"))
        x1Th_ready, x1Tl_ready = sem("x1Th_ready"), sem("x1Tl_ready")
        x1h_ready, x1l_ready = sem("x1h_ready"), sem("x1l_ready")
        zh_ready, zl_ready, qt_ready, qh_ready, ql_ready = (sem(n) for n in ("zh_ready", "zl_ready", "qt_ready", "qh_ready", "ql_ready"))
        out_ready = sem("out_ready")

        psT = ps[:, 0:2, :].rearrange("p s (j n) -> p (s j) n", n=P)
        psZ = ps[:, 6, 0:64]
        psQ = ps[0:64, 7, 0:P]
        psM = ps[:, 7, P:2 * P]
        x1_src = m.x1_rows.rearrange("b c t -> (b c) t")
        out_dst = out.rearrange("b c t -> (b c) t")

        def turns(eng, body):
            body(0, True, False)
            with eng.Fori(1, TURNS - 1) as i:
                body(i, False, False)
            body(TURNS - 1, False, True)

        with nc.Block() as block:
            @block.sync
            def _(sp):
                def load(p, u):
                    sp.dma_start(m.xt[:, u, :], x1_src[bass.ds(p * P, P), :]).then_inc(x1_loaded[u], 16)

                def store(p, u):
                    sp.wait_ge(out_ready, p + 1)
                    sp.dma_start(out_dst[bass.ds(p * P, P), :], m.outt[:, u % 2, :]).then_inc(out_stored[u % 2], 16)

                def body(i, first, last):
                    for u in range(U):
                        p = i * U + u
                        if not (last and u):
                            if not (first and u == 0):
                                sp.wait_ge(x1l_ready, p)
                            load(p + 3, (u + 3) % U)
                        if not (first and u < 2):
                            store(p - 2, u)

                for p in range(3):
                    load(p, p)
                turns(sp, body)
                store(Q - 2, 0)
                store(Q - 1, 1)
                for u in range(2):
                    sp.wait_ge(out_stored[u], 16 * (Q // 2))

            @block.gpsimd
            def _(gp):
                GP.memset(m.qt[:], 0.0).then_inc(cleared, 1)
                GP.memset(m.mp[:], 0.0).then_inc(cleared, 1)
                gp.wait_ge(cleared, 2)
                for slot in range(2):
                    for copy in range(2):
                        for b in range(2):
                            GP.tensor_copy(m.mp[32 * b:32 * b + 32, slot, copy, 32 * b:32 * b + R],
                                           ident[32 * b:32 * b + 32, 32 * b:32 * b + R]).then_inc(cleared, 1)
                gp.wait_ge(cleared, 10)

                def body(i, first, last):
                    for u in range(U):
                        p = i * U + u
                        if not first:
                            gp.wait_ge(o_done, p - U + 1)
                        GP.tensor_copy(m.idx_now[:, u, 0:1], m.idx_a[:, bass.ds(p, 1)]).then_inc(a_idx, 1)
                        gp.wait_ge(a_idx, p + 1)
                        gp.sem_inc(held_gather, 1)
                        gp.indirect_dma_start(m.asel[:, u, :], None, m.a_rows,
                                              bass.IndirectOffsetOnAxis(ap=m.idx_now[:, u, 0:1], axis=0)).then_inc(a_gathered[u], 16)
                        if not (first and u < 2):
                            gp.wait_ge(mq_done, p - 1)
                        for copy in range(2):
                            GP.tensor_copy(m.mp[:, u % 2, copy, :].rearrange("p (b l r) -> p b l r", b=2, l=2)[:, :, 1, :],
                                           m.g_pairs[:, bass.ds(p, 1), :, :].rearrange("p o b r -> p (o b) r")).then_inc(m_selected, 1)

                turns(gp, body)

            @block.scalar
            def _(act):
                def high_turned(p, u):
                    act.wait_ge(turned_done, p + 1)
                    S.activation(m.x1T[:, 0, :, :], psT, ACT.Copy).then_inc(x1Th_ready, 1)

                def high(p, u, count):
                    act.wait_ge(x1_loaded[u % U], count)
                    S.activation(m.x1h[:, u % U, :], m.xt[:, u % U, :], ACT.Copy).then_inc(x1h_ready, 1)

                def body(i, first, last):
                    for u in range(U):
                        p = i * U + u
                        if not (first and u < 2):
                            act.wait_ge(o_done, p - 1)
                            if not (first and u < 4):
                                act.wait_ge(out_stored[u % 2], 16 * (2 * i + u // 2 - 1))
                            S.activation(m.outt[:, u % 2, :], ps[:, 2 + 2 * (u % 2):4 + 2 * (u % 2), :].rearrange("p s n -> p (s n)"),
                                         ACT.Identity, bias=m.bias_t[:, bass.ds(p - 2, 1)]).then_inc(out_ready, 1)
                        if not (last and u == 3):
                            high_turned(p + 1, u + 1)
                            high(p + 1, u + 1, 16 * (i + 1 + (u + 1) // U))
                        act.wait_ge(mq_done, p + 1)
                        S.activation(m.qh[:, u % 2, :], psM, ACT.Copy).then_inc(qh_ready, 1)

                high_turned(0, 0)
                high(0, 0, 16)
                turns(act, body)
                for u in range(2):
                    act.wait_ge(o_done, Q - 1 + u)
                    act.wait_ge(out_stored[u], 16 * (Q // 2 - 1))
                    S.activation(m.outt[:, u, :], ps[:, 2 + 2 * u:4 + 2 * u, :].rearrange("p s n -> p (s n)"),
                                 ACT.Identity, bias=m.bias_t[:, Q - 2 + u:Q - 1 + u]).then_inc(out_ready, 1)

            @block.vector
            def _(dve):
                def low_turned(p, u):
                    dve.wait_ge(x1Th_ready, p + 1)
                    V.tensor_tensor(m.x1T[:, 1, :, :], psT, m.x1T[:, 0, :, :], ALU.subtract).then_inc(x1Tl_ready, 1)

                def load_ids(p, pairs):
                    _, ids = nc.values_load_multi_w_load_instructions(
                        m.sel_ids[:].rearrange("o q b l -> o (q b l)")[:, bass.ds(4 * p, 4 * pairs)],
                        engines=(mybir.EngineType.DVE,), min_val=0, max_val=N2 - 1,
                        skip_runtime_bounds_check_because="an adapter's number is below the count of its table's adapters")
                    return ids

                def select(ids, u):
                    for n in range(4):
                        table = m.bt[:, N1:, :, :, :] if n % 2 else m.bt[:, 0:N2, :, :, :]
                        V.tensor_copy(m.bsel[:, u % 2, n, :, :, :].rearrange("p s j r -> p (s j r)"),
                                      table[:, bass.ds(ids[n], 1), :, :, :].rearrange("p o s j r -> p (o s j r)")).then_inc(b_selected, 1)

                def body(i, first, last):
                    ids = load_ids(U * i + 1, U - 1 if last else U)
                    for u in range(U):
                        p = i * U + u
                        dve.wait_ge(z_done, p + 1)
                        V.tensor_scalar(m.zh[:], psZ, 1 / A_SCALE, None, ALU.mult).then_inc(zh_ready, 1)
                        dve.wait_ge(zh_ready, p + 1)
                        V.scalar_tensor_tensor(m.zl[:], psZ, 1 / A_SCALE, m.zh[:], ALU.mult, ALU.subtract).then_inc(zl_ready, 1)
                        if not (last and u == 3):
                            select(ids[4 * u:4 * u + 4], u + 1)
                        dve.wait_ge(x1h_ready, p + 1)
                        V.tensor_tensor(m.x1l[:, u, :], m.xt[:, u, :], m.x1h[:, u, :], ALU.subtract).then_inc(x1l_ready, 1)
                        dve.wait_ge(qt_done, p + 1)
                        for b in range(2):
                            rows, part = slice(32 * b, 32 * b + 32), slice(64 * b, 64 * b + 64)
                            V.tensor_copy(m.qt[rows, part], psQ[rows, part]).then_inc(qt_ready, 1)
                        if not (last and u == 3):
                            low_turned(p + 1, u + 1)
                        dve.wait_ge(qh_ready, p + 1)
                        V.tensor_tensor(m.ql[:, u % 2, :], psM[0:64, :], m.qh[0:64, u % 2, :], ALU.subtract).then_inc(ql_ready, 1)

                dve.wait_ge(cleared, 10)
                select(load_ids(0, 1), 0)
                low_turned(0, 0)
                turns(dve, body)

            @block.tensor
            def _(pe):
                def turn(p, u, count):
                    pe.wait_ge(x1_loaded[u % U], count)
                    for j in range(J):
                        last = PE.transpose(psT[:, j, :], m.xt[:, u % U, j * P:(j + 1) * P], ident[:])
                    last.then_inc(turned_done, 1)

                def mix(p, u, bank, early):
                    if bank == 0:
                        pe.wait_ge(x1l_ready, p + 1)
                        if not early:
                            pe.wait_ge(out_ready, p - 1)
                    o = ps[:, 2 + 2 * (u % 2) + bank, :]
                    cut = slice(bank * 512, bank * 512 + 512)
                    for k, (w, xp) in enumerate(((m.iwh, m.x1h), (m.iwh, m.x1l), (m.iwl, m.x1h))):
                        PE.matmul(o, w[:, bass.ds(p, 1), :].rearrange("p o d -> p (o d)"), xp[:, u, cut], start=(k == 0), stop=False)

                def add_adapters(p, u, count):
                    pe.wait_ge(ql_ready, p + 1)
                    pe.wait_ge(a_gathered[u], count)
                    for bank in range(2):
                        o = ps[:, 2 + 2 * (u % 2) + bank, :]
                        cut = slice(bank * 512, bank * 512 + 512)
                        PE.matmul(o, m.qh[:, u % 2, :], m.asel[:, u, cut], start=False, stop=False)
                        last = PE.matmul(o, m.ql[:, u % 2, :], m.asel[0:64, u, cut], start=False, stop=True)
                    last.then_inc(o_done, 1)

                def body(i, first, last):
                    for u in range(U):
                        p = i * U + u
                        has_prev = not (first and u == 0)
                        pu = (u - 1) % U
                        pe.wait_ge(x1Tl_ready, p + 1)
                        pe.wait_ge(b_selected, 4 * p + 4)
                        for j in range(J):
                            for k, (a, b) in enumerate(((0, 0), (0, 1), (1, 0))):
                                done = PE.matmul(psZ, m.x1T[:, a, j, :], m.bsel[:, u % 2, :, b, j, :],
                                                 start=(j == 0 and k == 0), stop=(j == J - 1 and k == 2))
                        done.then_inc(z_done, 1)
                        if not (last and u == 3):
                            turn(p + 1, u + 1, 16 * (i + 1 + (u + 1) // U))
                        if has_prev:
                            mix(p - 1, pu, 0, first and u < 3)
                        pe.wait_ge(zl_ready, p + 1)
                        if has_prev:
                            pe.wait_ge(ql_ready, p)
                        for k, (z, w) in enumerate(((m.zh, m.iwh), (m.zh, m.iwl), (m.zl, m.iwh))):
                            done = PE.matmul(psQ, z[:], w[:, bass.ds(p, 1), :].rearrange("p o d -> p (o d)"), start=(k == 0), stop=(k == 2))
                        done.then_inc(qt_done, 1)
                        if has_prev:
                            mix(p - 1, pu, 1, False)
                        pe.wait_ge(qt_ready, 2 * p + 2)
                        pe.wait_ge(m_selected, 2 * p + 2)
                        PE.matmul(psM, m.mp[:, u % 2, :, :].rearrange("p c n -> p (c n)"), m.qt[:], start=True, stop=True).then_inc(mq_done, 1)
                        if has_prev:
                            add_adapters(p - 1, pu, 16 * (i + 1) if u else 16 * i)

                turn(0, 0, 16)
                turns(pe, body)
                mix(Q - 1, 3, 0, False)
                mix(Q - 1, 3, 1, False)
                add_adapters(Q - 1, 3, 16 * TURNS)


def program(nc, x, lens, id1, id2, id3, log_dt, C, log_A_real, A_imag, D, A1, B1, A2, B2, W, bias, out):
    with ExitStack() as ctx:
        m = storage(nc, ctx)
        setup_stage(nc, m, x, lens, id1, id2, id3, log_dt, C, log_A_real, A_imag, D, A1, B1, A2, B2, W, bias)
        channel_stage(nc, m, x, W)
        pair_stage(nc, m, out)


_INS = ['x', 'itok_B_8_3872', 'itok_B_3_7', 'itok_B_4_50', 'itok_B_0_31', 'L0_cond_log_dt', 'L0_cond_C', 'L0_cond_log_A_real',
        'L0_cond_A_imag', 'L0_cond_D', 'L1_cond_A', 'L1_cond_B', 'L2_cond_A', 'L2_cond_B', 'L3_cond_weights', 'L3_cond_biases']


def kernel(**inputs):
    import numpy as _np
    import concourse.bacc as _bacc
    from concourse import mybir as _mybir
    from concourse.bass_utils import run_bass_kernel_spmd as _run

    nc = _bacc.Bacc("TRN2", target_bir_lowering=False, num_devices=1)
    arrays, args = {}, []
    for name in _INS:
        a = _np.ascontiguousarray(inputs[name])
        arrays[f"in_{name}"] = a
        args.append(nc.dram_tensor(f"in_{name}", a.shape, _mybir.dt.from_np(a.dtype), kind="ExternalInput").ap())
    args.append(nc.dram_tensor("out_dram", inputs["x"].shape, F32, kind="ExternalOutput").ap())
    program(nc, *args)
    r = _run(nc, [arrays], core_ids=[0])
    return r.results[0]["out_dram"]
```

```python
from contextlib import ExitStack


import concourse.bass as bass
from concourse import mybir

F32 = mybir.dt.float32
F16 = mybir.dt.float16
I32 = mybir.dt.int32
U8 = mybir.dt.uint8
ALU = mybir.AluOpType
ACT = mybir.ActivationFunctionType

P = 128
B = 128
H = 64
L = 1024
J = L // P
N = 64
R = 16
N1, N2, NS = 8, 64, 32
Q = B // 2
G = 1 + N2 * R // P
TC = 32
KPAD = L + P
A_SCALE = 64.0
GROW = N1 * R * N2
U = 4

MAGIC = 12582912.0
LOG2E = 1.4426950408889634
LN2_HI, LN2_LO = 0.693359375, -2.12194440e-4
TURN = 6.2831853071795865
TWO_PI = 6.283185
PI_2 = 1.5707963267948966


class Storage:
    pass


def storage(nc, ctx):
    m = Storage()

    def sb(name, shape, dt):
        return ctx.enter_context(nc.sbuf_tensor(name, shape, dt))

    m.k_rows = nc.dram_tensor("k_rows", (H, 2, KPAD), F16).ap()
    m.x1_rows = nc.dram_tensor("x1_rows", (B, H, L), F32).ap()
    m.a_rows = nc.dram_tensor("a_rows", (2 * (N1 + N2) * R, L), F16).ap()
    m.g_rows = nc.dram_tensor("g_rows", (GROW + R, R), F32).ap()

    m.xt = sb("xt", [P, U, L], F32)
    m.toep = sb("toep", [P, U, 2, L], F16)
    m.xTh = sb("xTh", [P, 2, J, P], F16)
    m.xTl = sb("xTl", [P, 2, J, P], F16)
    m.bt = sb("bt", [P, N1 + N2, 2, J, R], F16)
    m.iwh = sb("iwh", [P, Q, P], F16)
    m.iwl = sb("iwl", [P, Q, P], F16)
    m.g_pairs = sb("g_pairs", [64, Q, 2, R], F32)
    m.own = sb("own", [P, 2, H], F32)
    m.own_g = sb("own_g", [64, 2, R], F32)
    m.mask = sb("mask", [P, L], U8)
    m.ident = sb("ident", [P, P], F32)
    m.eye2 = sb("eye2", [P, H], F32)
    m.x1h = sb("x1h", [P, U, L], F16)
    m.x1l = sb("x1l", [P, U, L], F16)
    m.bsel = sb("bsel", [P, 2, 4, 2, J, R], F16)
    m.asel = sb("asel", [P, U, L], F16)
    m.outt = sb("outt", [P, 2, L], F32)
    m.ids = sb("ids", [P, 4, B], I32)
    m.sel_ids = sb("sel_ids", [1, Q, 2, 2], I32)
    m.idx_a = sb("idx_a", [P, Q], I32)
    m.idx_g = sb("idx_g", [P, Q], I32)
    m.idx_w = sb("idx_w", [P, Q], I32)
    m.idx_now = sb("idx_now", [P, U, 2], I32)
    m.bias_t = sb("bias_t", [P, Q], F32)
    m.zh = sb("zh", [P, 64], F16)
    m.zl = sb("zl", [P, 64], F16)
    m.qt = sb("qt", [64, P], F32)
    m.mp = sb("mp", [64, 2, 2, 64], F32)
    m.qh = sb("qh", [P, 2, P], F16)
    m.ql = sb("ql", [64, 2, P], F16)
    m.wnow = sb("wnow", [P, 2, H], F32)
    m.wboth = sb("wboth", [P, 2, P], F32)
    m.gnow = sb("gnow", [64, 2, R], F32)
    m.ps = ctx.enter_context(nc.psum_tensor("ps", [P, 8, 512], F32))
    return m


def natural_b(m):
    return m.bsel[:].rearrange("p a b c d e -> p (a b c d e)").bitcast(F32)


def transposed_a(m):
    return m.asel[:, 0:2, :], m.asel[:, 2:4, :].rearrange("p s (j n) -> p s j n", j=J)


def by_adapter(turned):
    return turned.rearrange("p j (a r) -> p a j r", r=R)


def group_rows(m):
    return m.a_rows.rearrange("(s n) t -> n s t", s=2)


def setup_stage(nc, m, x, lens, id1, id2, id3, log_dt, C, log_A_real, A_imag, D, A1, B1, bias):
    ps, ident = m.ps, m.ident
    V, S, PE = nc.vector, nc.scalar, nc.tensor
    with ExitStack() as ctx:
        def sb(name, shape, dt):
            return ctx.enter_context(nc.sbuf_tensor(name, shape, dt))

        def sem(name):
            return ctx.enter_context(nc.semaphore(name))

        logs = sb("logs", [H, 72], F32)
        aim = sb("aim", [H, N], F32)
        cri = sb("cri", [H, N, 2], F32)
        work = sb("work", [H, 19, 72], F32)
        pow2 = sb("pow2", [H, 72], I32)
        packed = sb("packed", [H, 4, P], F32)
        par = sb("par", [P, 4, H], F32)
        step = sb("step", [P, 2, TC], F32)
        k0add = sb("k0add", [P, 16], F32)
        khl = sb("khl", [P, 2, 512], F16)
        zeros = sb("zeros", [P, P], F16)
        biases = sb("biases", [NS, H], F32)
        onehot = sb("onehot", [NS, B], F32)
        idf = sb("idf", [P, 4, B], F32)
        lenc = sb("lenc", [P, 1], I32)
        lenf = sb("lenf", [P, 1], F32)
        coli = sb("coli", [P, 4], I32)
        colf = sb("colf", [P, 4], F32)
        cols = sb("cols", [P, 12], F32)
        tmp = sb("tmp", [P, 2, Q], F32)

        def halves(t):
            f = t.rearrange("p a b -> p (a b)").bitcast(F32)
            return f[:, 0:H * TC], f[:, H * TC:2 * H * TC]

        turns_v, turns_u = halves(m.iwh[:])
        decay_v, decay_u = halves(m.iwl[:])
        sin_u = m.x1h[:].rearrange("p a b -> p (a b)").bitcast(F32)
        cos_u = m.x1l[:].rearrange("p a b -> p (a b)").bitcast(F32)
        rounded_v = m.bt[:, N1:N1 + 16, :, :, :].rearrange("p a s j r -> p (a s j r)").bitcast(F32)
        a1f = m.outt[:, 0, :]
        iota_t = m.outt[:, 1, :]
        iota_i = m.bsel[:].rearrange("p a b c d e -> p (a b c d e)").bitcast(I32)
        nat_b = natural_b(m)
        nat_a, by_k, kf = (m.toep[:, n, :, :].rearrange("p a b -> p (a b)").bitcast(F32) for n in range(3))
        kf = kf[:, 0:512]
        at, a1c = transposed_a(m)

        def over_h(t):
            return t.rearrange("p (h c) -> p h c", c=TC)

        def blocks(k):
            return ps[:, k:k + 2, :].rearrange("p s (j n) -> p (s j) n", n=P)

        logs_loaded, aim_loaded, c_loaded, d_loaded = (sem(n) for n in ("logs_loaded", "aim_loaded", "c_loaded", "d_loaded"))
        x_first = sem("x_first")
        ids_loaded = sem("ids_loaded")
        bias_loaded = sem("bias_loaded")
        const_made = sem("const_made")
        k0_cleared = sem("k0_cleared")
        iota_made = sem("iota_made")
        dve_step = sem("dve_step")
        angle_ready = sem("angle_ready")
        sine_ready = sem("sine_ready")
        packed_ready = sem("packed_ready")
        packed_turned = sem("packed_turned")
        par_ready = sem("par_ready")
        products = sem("products")
        decays = sem("decays")
        turns_v_ready, turns_u_ready = sem("turns_v_ready"), sem("turns_u_ready")
        v_ready = sem("v_ready")
        abs_u_ready = sem("abs_u_ready")
        trig_v, trig_s, trig_c = sem("trig_v"), sem("trig_s"), sem("trig_c")
        uv_ready = sem("uv_ready")
        k_done = sem("k_done")
        khl_ready = sem("khl_ready")
        k_stored = sem("k_stored")
        onehot_ready, bias_done = sem("onehot_ready"), sem("bias_done")
        b_loaded, a_loaded = sem("b_loaded"), sem("a_loaded")
        a_ordered = sem("a_ordered")
        b_turned, a_turned = sem("b_turned"), sem("a_turned")
        b_high, b_low, a_high, a_low = sem("b_high"), sem("b_low"), sem("a_high"), sem("a_low")
        a_stored = sem("a_stored")
        a1_copied, a1_back, a1_high, a1_low = sem("a1_copied"), sem("a1_back"), sem("a1_high"), sem("a1_low")
        g_stored = sem("g_stored")

        with nc.Block() as block:
            @block.sync
            def _(sp):
                sp.dma_start(logs[:, 0:64], log_A_real).then_inc(logs_loaded, 16)
                sp.dma_start(logs[:, 64:65], log_dt.rearrange("(h o) -> h o", o=1)).then_inc(logs_loaded, 16)
                sp.dma_start(aim[:], A_imag).then_inc(aim_loaded, 16)
                sp.dma_start(cri[:], C).then_inc(c_loaded, 16)
                sp.dma_start(nat_a.rearrange("p (a n) -> p a n", a=8), A1.rearrange("a (p k) r -> p a (k r)", k=J)).then_inc(a_loaded, 16)
                sp.wait_ge(iota_made, 2)
                sp.dma_start(nat_b, B1.rearrange("a r t -> (a r) t")).then_inc(b_loaded, 16)
                sp.wait_ge(k0_cleared, 1)
                sp.dma_start(k0add[TC - 1:P:TC, :], D.rearrange("(q j) -> q j", j=16)).then_inc(d_loaded, 16)
                sp.dma_start(lenc[:], lens.rearrange("(b o) -> b o", o=1)).then_inc(ids_loaded, 16)
                for n, v in enumerate((lens, id1, id2, id3)):
                    sp.dma_start(m.ids[:, n, :], v.rearrange("(o b) -> o b", o=1).broadcast_to([P, B])).then_inc(ids_loaded, 16)
                sp.dma_start(biases[:], bias.rearrange("s o d -> s (o d)")).then_inc(bias_loaded, 16)
                for h in range(3):
                    sp.dma_start(m.xt[:, h, :], x[:, h, :]).then_inc(x_first, 16)
                sp.wait_ge(const_made, 4)
                sp.dma_start(m.k_rows[:, :, L:].rearrange("h s z -> (h s) z"), zeros[:]).then_inc(k_stored, 16)
                sp.dma_start(m.g_rows[GROW:GROW + R, :], ident[0:R, 0:R]).then_inc(g_stored, 16)
                sp.wait_ge(khl_ready, 1)
                for q in range(4):
                    for part in range(2):
                        sp.dma_start(
                            m.k_rows[16 * q:16 * q + 16, part, 0:L].rearrange("h (a c) -> a h c", c=TC),
                            khl[32 * q:32 * q + 32, part, :].rearrange("a (h c) -> a h c", c=TC)).then_inc(k_stored, 16)
                sp.wait_ge(a_low, 1)
                sp.dma_start(group_rows(m)[0:P, :, :], at).then_inc(a_stored, 16)
                sp.wait_ge(g_stored, 16)
                sp.wait_ge(a_stored, 16)
                sp.wait_ge(x_first, 48)
                sp.wait_ge(k_stored, 16 * 9)

            @block.gpsimd
            def _(gp):
                gp.memset(k0add[:], 0.0).then_inc(k0_cleared, 1)
                gp.memset(ident[:], 0.0).then_inc(const_made, 1)
                gp.wait_ge(const_made, 1)
                gp.affine_select(out=ident[:], in_=ident[:], compare_op=ALU.not_equal, fill=1.0, base=0,
                                 pattern=[[-1, P]], channel_multiplier=1).then_inc(const_made, 1)
                gp.iota(iota_i, pattern=[[1, L]], base=0, channel_multiplier=0).then_inc(iota_made, 1)
                gp.iota(coli[:, 0:1], pattern=[[0, 1]], base=0, channel_multiplier=1).then_inc(const_made, 1)
                gp.memset(zeros[:], 0.0).then_inc(const_made, 1)
                gp.wait_ge(a_loaded, 16)
                gp.tensor_copy(by_k.rearrange("p (k a r) -> p k a r", k=J, a=8),
                               nat_a.rearrange("p (a k r) -> p k a r", a=8, k=J)).then_inc(a_ordered, 1)
                gp.wait_ge(par_ready, 1)
                for dst, s in ((decay_v, 0), (decay_u, 1)):
                    gp.tensor_tensor(over_h(dst), par[:, 0, :].unsqueeze(2).broadcast_to([P, H, TC]),
                                     step[:, s, :].unsqueeze(1).broadcast_to([P, H, TC]), ALU.mult).then_inc(products, 1)
                gp.wait_ge(trig_v, 1)
                gp.wait_ge(decays, 1)
                gp.tensor_tensor(turns_v, turns_v, decay_v, ALU.mult).then_inc(v_ready, 1)

            @block.scalar
            def _(act):
                act.wait_ge(angle_ready, 1)
                S.activation(work[:, 10, 0:64], work[:, 9, 0:64], ACT.Sin, scale=TWO_PI).then_inc(sine_ready, 1)
                S.activation(work[:, 11, 0:64], work[:, 9, 0:64], ACT.Sin, scale=TWO_PI / 2).then_inc(sine_ready, 1)
                act.wait_ge(b_turned, 1)
                S.activation(m.bt[:, 0:N1, 0, :, :], by_adapter(blocks(2)), ACT.Copy).then_inc(b_high, 1)
                act.wait_ge(a_turned, 1)
                S.activation(at[:, 0, :].rearrange("p (t k) -> p t k", k=J),
                             blocks(4).rearrange("p k t -> p t k"), ACT.Copy, scale=A_SCALE).then_inc(a_high, 1)
                act.wait_ge(products, 1)
                S.activation(decay_v, decay_v, ACT.Exp).then_inc(decays, 1)
                act.wait_ge(turns_u_ready, 1)
                S.activation(cos_u, turns_u, ACT.Abs).then_inc(abs_u_ready, 1)
                act.wait_ge(products, 2)
                S.activation(decay_u, decay_u, ACT.Exp).then_inc(decays, 1)
                S.activation(sin_u, turns_u, ACT.Sin, scale=-TWO_PI).then_inc(trig_s, 1)
                act.wait_ge(abs_u_ready, 1)
                S.activation(cos_u, cos_u, ACT.Sin, scale=-TWO_PI, bias=cols[:, 2:3]).then_inc(trig_c, 1)
                act.wait_ge(turns_v_ready, 1)
                S.activation(turns_v, turns_v, ACT.Sin, scale=-TWO_PI, bias=cols[:, 1:2]).then_inc(trig_v, 1)
                act.wait_ge(a1_back, 1)
                S.activation(a1c[:, 0, :, :], blocks(6), ACT.Copy, scale=A_SCALE).then_inc(a1_high, 1)

            @block.tensor
            def _(pe):
                pe.wait_ge(const_made, 2)
                pe.wait_ge(b_loaded, 16)
                for j in range(J):
                    last = PE.transpose(blocks(2)[:, j, :], nat_b[:, j * P:(j + 1) * P], ident[:])
                last.then_inc(b_turned, 1)
                pe.wait_ge(a_ordered, 1)
                for k in range(J):
                    last = PE.transpose(blocks(4)[:, k, :], by_k[:, k * P:(k + 1) * P], ident[:])
                last.then_inc(a_turned, 1)
                pe.wait_ge(packed_ready, 1)
                for n in range(4):
                    last = PE.transpose(ps[:, 1, n * H:(n + 1) * H], packed[:, n, :], ident[0:H, 0:H])
                last.then_inc(packed_turned, 1)
                pe.wait_ge(v_ready, 1)
                for h in range(H):
                    q, j = h // 16, h % 16
                    if j == 0 and q % 2 == 0:
                        pe.wait_ge(uv_ready, q // 2 + 1)
                    last = PE.matmul(ps[32 * q:32 * q + 32, 0, j * TC:(j + 1) * TC], over_h(cos_u)[:, h, :],
                                     over_h(turns_v)[:, h, :], start=True, stop=True)
                last.then_inc(k_done, 1)
                pe.wait_ge(a1_copied, 1)
                for j in range(J):
                    last = PE.transpose(blocks(6)[:, j, :], a1f[:, j * P:(j + 1) * P], ident[:])
                last.then_inc(a1_back, 1)
                pe.wait_ge(bias_loaded, 16)
                pe.wait_ge(onehot_ready, 1)
                for b in range(2):
                    last = PE.matmul(ps[64 * b:64 * b + 64, 1, 256:256 + Q], biases[:],
                                     onehot[:].rearrange("s (q b) -> s b q", b=2)[:, b, :], start=True, stop=True)
                last.then_inc(bias_done, 1)

            @block.vector
            def _(dve):
                steps = [0]

                def step_of(ins):
                    ins.then_inc(dve_step, 1)
                    steps[0] += 1

                def settle():
                    dve.wait_ge(dve_step, steps[0])

                def link(ins):
                    step_of(ins)
                    settle()

                def t(n, w=64):
                    return work[:, n, 0:w]

                def exp_parts(src, w):
                    k, r, e = t(0, w), t(1, w), t(2, w)
                    link(V.tensor_scalar(k, src, LOG2E, MAGIC, ALU.mult, ALU.add))
                    link(V.tensor_scalar(k, k, MAGIC, -126.0, ALU.subtract, ALU.max))
                    step_of(V.tensor_scalar(pow2[:, 0:w], k, 127.0, 8388608.0, ALU.add, ALU.mult))
                    link(V.scalar_tensor_tensor(r, k, -LN2_HI, src, ALU.mult, ALU.add))
                    step_of(V.tensor_copy(t(3, w), pow2[:, 0:w].bitcast(F32)))
                    link(V.scalar_tensor_tensor(r, k, -LN2_LO, r, ALU.mult, ALU.add))
                    link(V.tensor_scalar(e, r, 1 / 5040, None, ALU.mult))
                    for c in (1 / 720, 1 / 120, 1 / 24, 1 / 6, 1 / 2, 1.0):
                        link(V.scalar_tensor_tensor(e, e, c, r, ALU.add, ALU.mult))

                dve.wait_ge(iota_made, 1)
                V.tensor_copy(iota_t, iota_i).then_inc(iota_made, 1)
                dve.wait_ge(iota_made, 2)
                step_of(V.memset(cols[0:64, 1:2], PI_2))
                step_of(V.memset(cols[64:128, 1:2], 0.0))
                step_of(V.memset(cols[:, 2:3], PI_2))
                step_of(V.tensor_scalar(step[:, 0, :], iota_t[:, 0:TC], -1.0, TC - 1.0, ALU.mult, ALU.add))

                dve.wait_ge(logs_loaded, 32)
                exp_parts(logs[:, 0:65], 65)
                link(V.scalar_tensor_tensor(t(4, 65), t(2, 65), 1.0, t(3, 65), ALU.add, ALU.mult))
                nar, dt = t(4), work[:, 4, 64:65]
                dve.wait_ge(aim_loaded, 16)
                step_of(V.tensor_scalar(t(6), aim[:], dt, 1 / TURN, ALU.mult, ALU.mult))
                step_of(V.tensor_scalar(t(5), nar, dt, -1.0, ALU.mult, ALU.mult))
                step_of(V.tensor_tensor(t(17), nar, nar, ALU.mult))
                step_of(V.tensor_tensor(t(18), aim[:], aim[:], ALU.mult))
                link(V.tensor_scalar(step[:, 1, :], step[:, 0, :], float(TC), None, ALU.mult))
                step_of(V.tensor_scalar(t(7), t(6), MAGIC, None, ALU.add))
                link(V.tensor_tensor(t(17), t(17), t(18), ALU.add))
                step_of(V.tensor_scalar(t(8), t(7), MAGIC, None, ALU.subtract))
                link(V.reciprocal(t(17), t(17)))
                V.tensor_tensor(t(9), t(6), t(8), ALU.subtract).then_inc(angle_ready, 1)
                for half in (slice(0, 64), slice(64, 128)):
                    step_of(V.tensor_copy(packed[:, 0, half], t(5)))
                    step_of(V.tensor_copy(packed[:, 1, half], t(6)))
                exp_parts(t(5), 64)
                link(V.tensor_tensor(t(0), t(2), t(3), ALU.mult))
                link(V.scalar_tensor_tensor(t(1), t(3), -1.0, t(0), ALU.add, ALU.add))
                dve.wait_ge(sine_ready, 2)
                step_of(V.tensor_tensor(t(8), t(11), t(11), ALU.mult))
                link(V.tensor_scalar(t(2), t(1), 1.0, None, ALU.add))
                step_of(V.tensor_tensor(t(7), t(2), t(10), ALU.mult))
                link(V.tensor_tensor(t(8), t(8), t(2), ALU.mult))
                step_of(V.tensor_tensor(t(3), t(7), aim[:], ALU.mult))
                step_of(V.tensor_tensor(t(15), t(7), nar, ALU.mult))
                link(V.scalar_tensor_tensor(t(12), t(8), -2.0, t(1), ALU.mult, ALU.add))
                step_of(V.tensor_tensor(t(2), t(12), nar, ALU.mult))
                link(V.tensor_tensor(t(16), t(12), aim[:], ALU.mult))
                step_of(V.tensor_tensor(t(13), t(3), t(2), ALU.subtract))
                link(V.tensor_tensor(t(14), t(15), t(16), ALU.add))
                step_of(V.scalar_tensor_tensor(t(13), t(13), 2.0, t(17), ALU.mult, ALU.mult))
                link(V.scalar_tensor_tensor(t(14), t(14), -2.0, t(17), ALU.mult, ALU.mult))
                dve.wait_ge(c_loaded, 16)
                cr, ci = cri[:, :, 0], cri[:, :, 1]
                step_of(V.tensor_tensor(t(0), cr, t(13), ALU.mult))
                step_of(V.tensor_tensor(t(1), ci, t(14), ALU.mult))
                step_of(V.tensor_tensor(t(2), cr, t(14), ALU.mult))
                link(V.tensor_tensor(t(3), ci, t(13), ALU.mult))
                step_of(V.tensor_tensor(packed[:, 2, 0:64], t(0), t(1), ALU.subtract))
                step_of(V.scalar_tensor_tensor(packed[:, 2, 64:128], t(2), -1.0, t(3), ALU.mult, ALU.subtract))
                step_of(V.tensor_tensor(packed[:, 3, 0:64], t(2), t(3), ALU.add))
                link(V.tensor_tensor(packed[:, 3, 64:128], t(0), t(1), ALU.subtract))
                dve.sem_inc(packed_ready, 1)
                dve.wait_ge(packed_turned, 1)
                V.tensor_copy(par[:], ps[:, 1, 0:4 * H].rearrange("p (n h) -> p n h", n=4)).then_inc(par_ready, 1)
                dve.wait_ge(par_ready, 1)

                def product(dst, s):
                    link(V.tensor_tensor(over_h(dst), par[:, 1, :].unsqueeze(2).broadcast_to([P, H, TC]),
                                         step[:, s, :].unsqueeze(1).broadcast_to([P, H, TC]), ALU.mult))

                product(turns_u, 1)
                link(V.tensor_scalar(cos_u, turns_u, MAGIC, None, ALU.add))
                V.scalar_tensor_tensor(turns_u, cos_u, MAGIC, turns_u, ALU.subtract, ALU.subtract).then_inc(turns_u_ready, 1)
                product(turns_v, 0)
                link(V.tensor_scalar(rounded_v, turns_v, MAGIC, None, ALU.add))
                link(V.scalar_tensor_tensor(turns_v, rounded_v, MAGIC, turns_v, ALU.subtract, ALU.subtract))
                V.scalar_tensor_tensor(turns_v[0:64, :], turns_v[0:64, :], -1.0, turns_v[0:64, :], ALU.mult, ALU.max).then_inc(turns_v_ready, 1)
                dve.wait_ge(turns_v_ready, 1)
                for half in range(2):
                    hs = slice(half * H // 2, (half + 1) * H // 2)
                    cut = slice(half * H // 2 * TC, (half + 1) * H // 2 * TC)

                    def coefficient(n):
                        return par[:, n, hs].unsqueeze(2).broadcast_to([P, H // 2, TC])

                    if half == 0:
                        dve.wait_ge(trig_s, 1)
                    step_of(V.tensor_tensor(over_h(sin_u)[:, hs, :], over_h(sin_u)[:, hs, :], coefficient(3), ALU.mult))
                    if half == 0:
                        dve.wait_ge(trig_c, 1)
                    link(V.tensor_tensor(over_h(cos_u)[:, hs, :], over_h(cos_u)[:, hs, :], coefficient(2), ALU.mult))
                    link(V.tensor_tensor(cos_u[:, cut], cos_u[:, cut], sin_u[:, cut], ALU.subtract))
                    if half == 0:
                        dve.wait_ge(decays, 2)
                    V.tensor_tensor(cos_u[:, cut], cos_u[:, cut], decay_u[:, cut], ALU.mult).then_inc(uv_ready, 1)

                dve.wait_ge(b_high, 1)
                V.tensor_tensor(m.bt[:, 0:N1, 1, :, :], by_adapter(blocks(2)), m.bt[:, 0:N1, 0, :, :], ALU.subtract).then_inc(b_low, 1)
                dve.wait_ge(a_high, 1)
                turned = blocks(4).rearrange("p k t -> p t k")
                V.tensor_copy(a1f.rearrange("p (t k) -> p t k", k=J), turned).then_inc(a1_copied, 1)
                V.scalar_tensor_tensor(at[:, 1, :].rearrange("p (t k) -> p t k", k=J), turned, A_SCALE,
                                       at[:, 0, :].rearrange("p (t k) -> p t k", k=J), ALU.mult, ALU.subtract).then_inc(a_low, 1)

                dve.wait_ge(const_made, 3)
                link(V.tensor_scalar(coli[:, 1:2], coli[:, 0:1], TC - 1, None, ALU.bitwise_and))
                link(V.tensor_copy(cols[:, 10:11], coli[:, 1:2]))
                link(V.tensor_scalar(cols[:, 10:11], cols[:, 10:11], TC - 1.0, None, ALU.is_equal))
                dve.wait_ge(d_loaded, 16)
                link(V.tensor_scalar(k0add[:], k0add[:], cols[:, 10:11], None, ALU.add))
                dve.wait_ge(k_done, 1)
                link(V.tensor_copy(kf, ps[:, 0, :]))
                k0 = over_h(kf)[:, :, TC - 1]
                link(V.tensor_tensor(k0, k0, k0add[:], ALU.add))
                link(V.tensor_copy(khl[:, 0, :], kf))
                V.tensor_tensor(khl[:, 1, :], kf, khl[:, 0, :], ALU.subtract).then_inc(khl_ready, 1)

                dve.wait_ge(ids_loaded, 80)
                step_of(V.tensor_copy(idf[:], m.ids[:]))
                step_of(V.tensor_copy(lenf[:], lenc[:]))
                step_of(V.tensor_scalar(coli[:, 1:2], coli[:, 0:1], 4, 1, ALU.logical_shift_right, ALU.bitwise_and))
                step_of(V.tensor_scalar(coli[:, 2:3], coli[:, 0:1], 15, None, ALU.bitwise_and))
                link(V.tensor_scalar(coli[:, 3:4], coli[:, 0:1], 6, None, ALU.logical_shift_right))
                step_of(V.tensor_scalar(m.mask[:], iota_t, lenf[:, 0:1], None, ALU.is_lt))
                link(V.tensor_copy(colf[:], coli[:]))
                pf, lf, rf, sf = (colf[:, n:n + 1] for n in range(4))
                V.tensor_scalar(onehot[:], idf[0:NS, 3, :], pf[0:NS, :], None, ALU.is_equal).then_inc(onehot_ready, 1)

                def col(n, rows=slice(0, P)):
                    return cols[rows, n:n + 1]

                step_of(V.tensor_scalar(col(3), lf, -1.0, 1.0, ALU.mult, ALU.add))
                step_of(V.tensor_scalar(col(5), lf, float(R), None, ALU.mult))
                step_of(V.scalar_tensor_tensor(col(9), sf, -64.0, pf, ALU.mult, ALU.add))
                link(V.scalar_tensor_tensor(col(6), sf, float((N1 + N2) * R), rf, ALU.mult, ALU.add))
                step_of(V.tensor_scalar(col(4), col(3), float(R), None, ALU.mult))
                step_of(V.scalar_tensor_tensor(col(6), lf, float(N1 * R), col(6), ALU.mult, ALU.add))
                step_of(V.tensor_scalar(col(7), col(3), float(R * N2), None, ALU.mult))
                link(V.scalar_tensor_tensor(col(8), col(3), float(N2), lf, ALU.mult, ALU.add))
                link(V.tensor_tensor(col(8), col(8), rf, ALU.mult))
                link(V.scalar_tensor_tensor(col(8), lf, float(GROW), col(8), ALU.mult, ALU.add))
                pair = idf[:].rearrange("p n (q b) -> p n b q", b=2)
                for k in range(4):
                    rows, b = slice(32 * k, 32 * k + 32), k % 2
                    step_of(V.tensor_scalar(tmp[rows, 0, :], pair[rows, 1, b, :], col(4, rows), col(6, rows), ALU.mult, ALU.add))
                    step_of(V.tensor_scalar(tmp[rows, 1, :], pair[rows, 1, b, :], col(7, rows), col(8, rows), ALU.mult, ALU.add))
                settle()
                for k in range(4):
                    rows, b = slice(32 * k, 32 * k + 32), k % 2
                    step_of(V.scalar_tensor_tensor(m.idx_a[rows, :], pair[rows, 2, b, :], col(5, rows), tmp[rows, 0, :], ALU.mult, ALU.add))
                    step_of(V.scalar_tensor_tensor(m.idx_g[rows, :], pair[rows, 2, b, :], col(3, rows), tmp[rows, 1, :], ALU.mult, ALU.add))
                step_of(V.memset(m.own[:], 0.0))
                step_of(V.memset(m.own_g[:], 0.0))
                settle()
                for b in range(2):
                    rows = slice(64 * b, 64 * b + 64)
                    step_of(V.tensor_scalar(m.idx_w[rows, :], pair[rows, 3, b, :], float(H), col(9, rows), ALU.mult, ALU.add))
                    step_of(V.tensor_copy(m.eye2[rows, :], ident[rows, 64 * b:64 * b + 64]))
                    step_of(V.memset(m.own[rows, b, :], 1.0))
                    step_of(V.memset(m.own_g[32 * b:32 * b + 32, b, :], 1.0))
                for layer in range(2):
                    step_of(V.tensor_copy(m.sel_ids[:, :, :, layer], m.ids[0:1, 1 + layer, :].rearrange("o (q b) -> o q b", b=2)))
                dve.wait_ge(a1_high, 1)
                V.scalar_tensor_tensor(a1c[:, 1, :, :], blocks(6), A_SCALE, a1c[:, 0, :, :], ALU.mult, ALU.subtract).then_inc(a1_low, 1)
                dve.wait_ge(bias_done, 1)
                link(V.tensor_copy(m.bias_t[:], ps[:, 1, 256:256 + Q]))
                dve.wait_ge(a1_low, 1)
                dve.wait_ge(b_low, 1)


def channel_stage(nc, m, x, W, A2, B2):
    ps, ident = m.ps, m.ident
    V, S, PE, GP = nc.vector, nc.scalar, nc.tensor, nc.gpsimd
    TURNS = H // U
    with ExitStack() as ctx:
        def sem(name):
            return ctx.enter_context(nc.semaphore(name))

        x_loaded = [sem(f"x_loaded{u}") for u in range(U)]
        toep_loaded = [sem(f"toep_loaded{u}") for u in range(U)]
        x1_stored = [sem(f"x1_stored{u}") for u in range(U)]
        xT_done = sem("xT_done")
        xTh_ready = sem("xTh_ready")
        xTl_ready = sem("xTl_ready")
        conv_done = sem("conv_done")
        x1_ready = sem("x1_ready")
        idx_copied = sem("idx_copied")
        held = sem("held")
        held_gather = sem("held_gather")
        w_gathered = [sem(f"w_gathered{u}") for u in range(2)]
        g_gathered = [sem(f"g_gathered{u}") for u in range(2)]
        w_both = sem("w_both")
        w_plus = sem("w_plus")
        w_high = sem("w_high")
        w_low = sem("w_low")
        g_kept = sem("g_kept")
        b_loaded, a_loaded, a_ordered = sem("b_loaded"), sem("a_loaded"), sem("a_ordered")
        b_turned, a_turned = sem("b_turned"), sem("a_turned")
        b_high, b_low, a_high, a_low = sem("b_high"), sem("b_low"), sem("a_high"), sem("a_low")
        a_stored, g_done, g_out_ready, g_stored = sem("a_stored"), sem("g_done"), sem("g_out_ready"), sem("g_stored")

        nat_b = natural_b(m)
        nat_a = m.outt[:, 0, :]
        by_k = m.outt[:, 1, :]
        at, a1c = transposed_a(m)
        g_out = m.x1h[:, 0, 0:2 * P].bitcast(F32)

        turned = ps[:, 0:2, :].rearrange("p s (j n) -> p (s j) n", n=P)
        group_turned = ps[:, 2:4, :].rearrange("p s (j n) -> p (s j) n", n=P)
        group_g = ps[:, 2, 0:P]

        def conv_out(h2):
            return ps[:, 4 + 2 * h2:6 + 2 * h2, :]

        def turns(eng, body):
            body(0, first=True, next_group=True)
            with eng.Fori(1, G - 1) as i:
                body(i, group=True, next_group=True)
            body(G - 1, group=True)
            with eng.Fori(G, TURNS - 1) as i:
                body(i)
            body(TURNS - 1, last=True)

        with nc.Block() as block:
            @block.sync
            def _(sp):
                def load_x(h, u):
                    sp.dma_start(m.xt[:, u, :], x[:, bass.ds(h, 1), :].rearrange("b o t -> b (o t)")).then_inc(x_loaded[u], 16)

                def load_toep(h, u):
                    row = bass.AP(m.k_rows.tensor, h * (2 * KPAD), [[1, P], [KPAD, 2], [1, L]])
                    sp.dma_start(m.toep[:, u, :, :], row).then_inc(toep_loaded[u], 16)

                def body(i, first=False, last=False, group=False, next_group=False):
                    for u in range(U):
                        h = i * U + u
                        sp.wait_ge(x1_ready, h + 1)
                        sp.dma_start(m.x1_rows[:, bass.ds(h, 1), :].rearrange("b o t -> b (o t)"), m.xt[:, u, :]).then_inc(x1_stored[u], 16)
                        if not (last and u):
                            v = (u + 3) % U
                            if not (first and u == 0):
                                sp.wait_ge(x1_stored[v], 16 * (i + (1 if u else 0)))
                            load_x(h + 3, v)
                            load_toep(h + 3, v)
                        if next_group and u == 2:
                            if group:
                                sp.wait_ge(b_turned, i)
                                sp.wait_ge(a_turned, i)
                            load_group(i + 1)
                    if group:
                        sp.wait_ge(g_out_ready, i)
                        rows = m.g_rows[0:GROW, :].rearrange("(n a) r -> n a r", n=P)
                        sp.dma_start(rows[:, bass.ds((i - 1) * 8, 8), :], g_out.rearrange("p (a r) -> p a r", r=R)).then_inc(g_stored, 16)
                        sp.dma_start(group_rows(m)[bass.ds(i * P, P), :, :], at).then_inc(a_stored, 16)

                def load_group(g):
                    sp.dma_start(nat_b, B2.rearrange("a r t -> (a r) t")[bass.ds((g - 1) * P, P), :]).then_inc(b_loaded, 16)
                    sp.dma_start(nat_a.rearrange("p (a n) -> p a n", a=8),
                                 A2.rearrange("a (p k) r -> p a (k r)", k=J)[:, bass.ds((g - 1) * 8, 8), :]).then_inc(a_loaded, 16)

                for h in range(3):
                    load_toep(h, h)
                turns(sp, body)
                sp.wait_ge(a_stored, 16 * (G - 1))
                for u in range(U):
                    sp.wait_ge(x1_stored[u], 16 * TURNS)

            @block.gpsimd
            def _(gp):
                w_src = W.rearrange("s c d -> (s c) d")

                def gather_w(q, v):
                    GP.tensor_copy(m.idx_now[:, v, 0:1], m.idx_w[:, bass.ds(q, 1)]).then_inc(idx_copied, 1)
                    gp.wait_ge(idx_copied, q + 1)
                    gp.sem_inc(held_gather, 1)
                    gp.indirect_dma_start(m.wnow[:, v, :], None, w_src,
                                          bass.IndirectOffsetOnAxis(ap=m.idx_now[:, v, 0:1], axis=0)).then_inc(w_gathered[v], 16)

                def keep_w(i, first=False, last=False):
                    for u in range(U):
                        q, v = i * U + u, u % 2
                        if not (last and u == 3):
                            if not (first and u == 0):
                                gp.wait_ge(w_both, q)
                            gather_w(q + 1, 1 - v)
                        gp.wait_ge(w_gathered[v], 16 * (2 * i + u // 2 + 1))
                        GP.tensor_tensor(m.wnow[:, v, :], m.wnow[:, v, :], m.eye2[:], ALU.add).then_inc(w_plus, 1)
                        gp.wait_ge(w_plus, q + 1)
                        both = m.wboth[:, v, :]
                        GP.tensor_tensor(both.rearrange("p (b d) -> p b d", b=2), m.wnow[:, v:v + 1, :].broadcast_to([P, 2, H]),
                                         m.own[:], ALU.mult).then_inc(w_both, 1)
                        gp.wait_ge(w_both, q + 1)
                        high = m.iwh[:, bass.ds(q, 1), :].rearrange("p o d -> p (o d)")
                        GP.tensor_copy(high, both).then_inc(w_high, 1)
                        gp.wait_ge(w_high, q + 1)
                        GP.tensor_tensor(m.iwl[:, bass.ds(q, 1), :].rearrange("p o d -> p (o d)"), both, high,
                                         ALU.subtract).then_inc(w_low, 1)

                def gather_g(q, v):
                    GP.tensor_copy(m.idx_now[:, v, 1:2], m.idx_g[:, bass.ds(q, 1)]).then_inc(idx_copied, 1)
                    gp.wait_ge(idx_copied, Q + q + 1)
                    gp.sem_inc(held_gather, 1)
                    gp.indirect_dma_start(m.gnow[:, v, :], None, m.g_rows,
                                          bass.IndirectOffsetOnAxis(ap=m.idx_now[0:64, v, 1:2], axis=0)).then_inc(g_gathered[v], 16)

                def keep_g(i, first=False, last=False):
                    for u in range(U):
                        q, v = i * U + u, u % 2
                        if not (last and u == 3):
                            if not (first and u == 0):
                                gp.wait_ge(g_kept, q)
                            gather_g(q + 1, 1 - v)
                        gp.wait_ge(g_gathered[v], 16 * (2 * i + u // 2 + 1))
                        GP.tensor_tensor(m.g_pairs[:, bass.ds(q, 1), :, :].rearrange("p o b r -> p (o b) r"),
                                         m.gnow[:, v:v + 1, :].broadcast_to([64, 2, R]), m.own_g[:], ALU.mult).then_inc(g_kept, 1)

                def all_pairs(gather, keep):
                    gather(0, 0)
                    keep(0, first=True)
                    with gp.Fori(1, TURNS - 1) as i:
                        keep(i)
                    keep(TURNS - 1, last=True)

                all_pairs(gather_w, keep_w)
                gp.wait_ge(g_stored, 16 * (G - 1))
                all_pairs(gather_g, keep_g)
                gp.wait_ge(w_low, Q)
                gp.wait_ge(g_kept, Q)

            @block.scalar
            def _(act):
                def body(i, first=False, last=False, group=False, next_group=False):
                    for u in range(U):
                        h = i * U + u
                        act.wait_ge(xT_done, h + 1)
                        if not (first and u < 2):
                            act.wait_ge(conv_done, h - 1)
                        S.activation(m.xTh[:, u % 2, :, :], turned, ACT.Copy).then_inc(xTh_ready, 1)
                        if group and u == 0:
                            act.wait_ge(a_loaded, 16 * i)
                            S.activation(by_k.rearrange("p (k a r) -> p k a r", k=J, a=8),
                                         nat_a.rearrange("p (a k r) -> p k a r", a=8, k=J), ACT.Copy).then_inc(a_ordered, 1)
                        if group and u == 1:
                            act.wait_ge(b_turned, i)
                            S.activation(m.bt[:, bass.ds(i * 8, 8), 0, :, :], by_adapter(group_turned), ACT.Copy).then_inc(b_high, 1)
                        if group and u == 2:
                            act.wait_ge(a_turned, i)
                            act.wait_ge(a_stored, 16 * i - 16)
                            S.activation(at[:, 0, :].rearrange("p (t k) -> p t k", k=J),
                                         group_turned.rearrange("p k t -> p t k"), ACT.Copy, scale=A_SCALE).then_inc(a_high, 1)
                        if group and u == 3:
                            act.wait_ge(g_done, i)
                            act.wait_ge(g_stored, 16 * i - 16)
                            S.activation(g_out, group_g, ACT.Copy, scale=1 / A_SCALE).then_inc(g_out_ready, 1)

                turns(act, body)

            @block.vector
            def _(dve):
                def low_part(h, u):
                    dve.wait_ge(xTh_ready, h + 1)
                    V.tensor_tensor(m.xTl[:, u % 2, :, :], turned, m.xTh[:, u % 2, :, :], ALU.subtract).then_inc(xTl_ready, 1)

                def body(i, first=False, last=False, group=False, next_group=False):
                    for u in range(U):
                        h = i * U + u
                        if not (last and u == 3):
                            low_part(h + 1, u + 1)
                        dve.wait_ge(conv_done, h + 1)
                        dve.sem_inc(held, 1)
                        V.copy_predicated(m.xt[:, u, :], m.mask[:], conv_out(u % 2).rearrange("p s n -> p (s n)")[:, ::-1]).then_inc(x1_ready, 1)
                        if group and u == 0:
                            dve.wait_ge(b_high, i)
                            cut = bass.ds(i * 8, 8)
                            V.tensor_tensor(m.bt[:, cut, 1, :, :], by_adapter(group_turned), m.bt[:, cut, 0, :, :], ALU.subtract).then_inc(b_low, 1)
                        if group and u == 1:
                            dve.wait_ge(a_high, i)
                            V.scalar_tensor_tensor(at[:, 1, :].rearrange("p (t k) -> p t k", k=J), group_turned.rearrange("p k t -> p t k"), A_SCALE,
                                                   at[:, 0, :].rearrange("p (t k) -> p t k", k=J), ALU.mult, ALU.subtract).then_inc(a_low, 1)

                low_part(0, 0)
                turns(dve, body)

            @block.tensor
            def _(pe):
                def turn(i, u, early):
                    h = i * U + u
                    if not (early and u < 3):
                        pe.wait_ge(x_loaded[u % U], 16 * (i + u // U + (1 if u == 3 else 0)))
                    if not (early and u == 0):
                        pe.wait_ge(xTl_ready, h)
                    for j in range(J):
                        last = PE.transpose(turned[:, j, :], m.xt[:, u % U, j * P:(j + 1) * P], ident[:])
                    last.then_inc(xT_done, 1)

                def convolve(i, u, early):
                    h = i * U + u
                    out = conv_out(u % 2)
                    pe.wait_ge(xTl_ready, h + 1)
                    pe.wait_ge(toep_loaded[u], 16 * (i + 1))
                    if not early:
                        pe.wait_ge(x1_ready, h - 1)
                    for j in range(J):
                        for k, (xT, part) in enumerate(((m.xTh, 0), (m.xTh, 1), (m.xTl, 0))):
                            for bank in range(2 if j < 4 else 1):
                                y0, y1 = bank * 512, min(bank * 512 + 512, L - j * P)
                                last = PE.matmul(out[:, bank, 0:y1 - y0], xT[:, u % 2, j, :],
                                                 m.toep[:, u, part, y0 + j * P:y1 + j * P],
                                                 start=(j == 0 and k == 0), stop=(j == 7 - 4 * bank and k == 2))
                    last.then_inc(conv_done, 1)

                def turn_b(g):
                    pe.wait_ge(b_loaded, 16 * g)
                    pe.wait_ge(g_out_ready, g - 1)
                    for j in range(J):
                        last = PE.transpose(group_turned[:, j, :], nat_b[:, j * P:(j + 1) * P], ident[:])
                    last.then_inc(b_turned, 1)

                def turn_a(g):
                    pe.wait_ge(a_ordered, g)
                    pe.wait_ge(b_low, g)
                    for k in range(J):
                        last = PE.transpose(group_turned[:, k, :], by_k[:, k * P:(k + 1) * P], ident[:])
                    last.then_inc(a_turned, 1)

                def join(g):
                    pe.wait_ge(a_low, g)
                    for j in range(J):
                        for k, (a, b) in enumerate(((0, 0), (0, 1), (1, 0))):
                            last = PE.matmul(group_g, a1c[:, a, j, :], m.bt[:, bass.ds(g * 8, 8), b, j, :],
                                             start=(j == 0 and k == 0), stop=(j == J - 1 and k == 2))
                    last.then_inc(g_done, 1)

                def body(i, first=False, last=False, group=False, next_group=False):
                    for u in range(U):
                        if not (last and u == 3):
                            turn(i, u + 1, first)
                        convolve(i, u, first and u < 2)
                        if group and u < 3:
                            (turn_b, turn_a, join)[u](i)

                turn(0, 0, True)
                turns(pe, body)


def pair_stage(nc, m, out):
    ps, ident = m.ps, m.ident
    V, S, PE, GP = nc.vector, nc.scalar, nc.tensor, nc.gpsimd
    TURNS = Q // U
    with ExitStack() as ctx:
        def sem(name):
            return ctx.enter_context(nc.semaphore(name))

        x1_loaded = [sem(f"x1_loaded{u}") for u in range(U)]
        a_gathered = [sem(f"a_gathered{u}") for u in range(U)]
        out_stored = [sem(f"out_stored{u}") for u in range(2)]
        cleared = sem("cleared")
        a_idx = sem("a_idx")
        held_gather = sem("held_gather")
        b_selected = sem("b_selected")
        m_selected = sem("m_selected")
        turned_done, z_done, qt_done, mq_done, o_done = (sem(n) for n in ("turned_done", "z_done", "qt_done", "mq_done", "o_done"))
        x1Th_ready, x1Tl_ready = sem("x1Th_ready"), sem("x1Tl_ready")
        x1h_ready, x1l_ready = sem("x1h_ready"), sem("x1l_ready")
        zh_ready, zl_ready, qt_ready, qh_ready, ql_ready = (sem(n) for n in ("zh_ready", "zl_ready", "qt_ready", "qh_ready", "ql_ready"))
        out_ready = sem("out_ready")

        psT = ps[:, 0:2, :].rearrange("p s (j n) -> p (s j) n", n=P)
        psZ = ps[:, 6, 0:64]
        psQ = ps[0:64, 7, 0:P]
        psM = ps[:, 7, P:2 * P]
        x1_src = m.x1_rows.rearrange("b c t -> (b c) t")
        out_dst = out.rearrange("b c t -> (b c) t")

        def turns(eng, body):
            body(0, True, False)
            with eng.Fori(1, TURNS - 1) as i:
                body(i, False, False)
            body(TURNS - 1, False, True)

        with nc.Block() as block:
            @block.sync
            def _(sp):
                def load(p, u):
                    sp.dma_start(m.xt[:, u, :], x1_src[bass.ds(p * P, P), :]).then_inc(x1_loaded[u], 16)

                def store(p, u):
                    sp.wait_ge(out_ready, p + 1)
                    sp.dma_start(out_dst[bass.ds(p * P, P), :], m.outt[:, u % 2, :]).then_inc(out_stored[u % 2], 16)

                def body(i, first, last):
                    for u in range(U):
                        p = i * U + u
                        if not (last and u):
                            if not (first and u == 0):
                                sp.wait_ge(x1l_ready, p)
                            load(p + 3, (u + 3) % U)
                        if not (first and u < 2):
                            store(p - 2, u)

                for p in range(3):
                    load(p, p)
                turns(sp, body)
                store(Q - 2, 0)
                store(Q - 1, 1)
                for u in range(2):
                    sp.wait_ge(out_stored[u], 16 * (Q // 2))

            @block.gpsimd
            def _(gp):
                GP.memset(m.qt[:], 0.0).then_inc(cleared, 1)
                GP.memset(m.mp[:], 0.0).then_inc(cleared, 1)
                gp.wait_ge(cleared, 2)
                for slot in range(2):
                    for copy in range(2):
                        for b in range(2):
                            GP.tensor_copy(m.mp[32 * b:32 * b + 32, slot, copy, 32 * b:32 * b + R],
                                           ident[32 * b:32 * b + 32, 32 * b:32 * b + R]).then_inc(cleared, 1)
                gp.wait_ge(cleared, 10)

                def body(i, first, last):
                    for u in range(U):
                        p = i * U + u
                        if not first:
                            gp.wait_ge(o_done, p - U + 1)
                        GP.tensor_copy(m.idx_now[:, u, 0:1], m.idx_a[:, bass.ds(p, 1)]).then_inc(a_idx, 1)
                        gp.wait_ge(a_idx, p + 1)
                        gp.sem_inc(held_gather, 1)
                        gp.indirect_dma_start(m.asel[:, u, :], None, m.a_rows,
                                              bass.IndirectOffsetOnAxis(ap=m.idx_now[:, u, 0:1], axis=0)).then_inc(a_gathered[u], 16)
                        if not (first and u < 2):
                            gp.wait_ge(mq_done, p - 1)
                        for copy in range(2):
                            GP.tensor_copy(m.mp[:, u % 2, copy, :].rearrange("p (b l r) -> p b l r", b=2, l=2)[:, :, 1, :],
                                           m.g_pairs[:, bass.ds(p, 1), :, :].rearrange("p o b r -> p (o b) r")).then_inc(m_selected, 1)

                turns(gp, body)

            @block.scalar
            def _(act):
                def high_turned(p, u):
                    act.wait_ge(turned_done, p + 1)
                    if u >= 2:
                        act.wait_ge(z_done, p - 1)
                    S.activation(m.xTh[:, u % 2, :, :], psT, ACT.Copy).then_inc(x1Th_ready, 1)

                def high(p, u, count):
                    act.wait_ge(x1_loaded[u % U], count)
                    S.activation(m.x1h[:, u % U, :], m.xt[:, u % U, :], ACT.Copy).then_inc(x1h_ready, 1)

                def body(i, first, last):
                    for u in range(U):
                        p = i * U + u
                        if not (first and u < 2):
                            act.wait_ge(o_done, p - 1)
                            if not (first and u < 4):
                                act.wait_ge(out_stored[u % 2], 16 * (2 * i + u // 2 - 1))
                            S.activation(m.outt[:, u % 2, :], ps[:, 2 + 2 * (u % 2):4 + 2 * (u % 2), :].rearrange("p s n -> p (s n)"),
                                         ACT.Identity, bias=m.bias_t[:, bass.ds(p - 2, 1)]).then_inc(out_ready, 1)
                        if not (first and u == 0):
                            high_q(p - 1, u - 1)
                        if not (last and u == 3):
                            high_turned(p + 1, (u + 1 if first else 2 + (u + 1) % 2))
                            high(p + 1, u + 1, 16 * (i + 1 + (u + 1) // U))

                def high_q(p, u):
                    act.wait_ge(mq_done, p + 1)
                    S.activation(m.qh[:, u % 2, :], psM, ACT.Copy).then_inc(qh_ready, 1)

                high_turned(0, 0)
                high(0, 0, 16)
                turns(act, body)
                high_q(Q - 1, 1)
                for u in range(2):
                    act.wait_ge(o_done, Q - 1 + u)
                    act.wait_ge(out_stored[u], 16 * (Q // 2 - 1))
                    S.activation(m.outt[:, u, :], ps[:, 2 + 2 * u:4 + 2 * u, :].rearrange("p s n -> p (s n)"),
                                 ACT.Identity, bias=m.bias_t[:, Q - 2 + u:Q - 1 + u]).then_inc(out_ready, 1)

            @block.vector
            def _(dve):
                def low_turned(p, u):
                    dve.wait_ge(x1Th_ready, p + 1)
                    V.tensor_tensor(m.xTl[:, u % 2, :, :], psT, m.xTh[:, u % 2, :, :], ALU.subtract).then_inc(x1Tl_ready, 1)

                def load_ids(p, pairs):
                    _, ids = nc.values_load_multi_w_load_instructions(
                        m.sel_ids[:].rearrange("o q b l -> o (q b l)")[:, bass.ds(4 * p, 4 * pairs)],
                        engines=(mybir.EngineType.DVE,), min_val=0, max_val=N2 - 1,
                        skip_runtime_bounds_check_because="an adapter's number is below the count of its table's adapters")
                    return ids

                def select(ids, u):
                    for n in range(4):
                        table = m.bt[:, N1:, :, :, :] if n % 2 else m.bt[:, 0:N2, :, :, :]
                        V.tensor_copy(m.bsel[:, u % 2, n, :, :, :].rearrange("p s j r -> p (s j r)"),
                                      table[:, bass.ds(ids[n], 1), :, :, :].rearrange("p o s j r -> p (o s j r)")).then_inc(b_selected, 1)

                def body(i, first, last):
                    for u in range(U):
                        p = i * U + u
                        dve.wait_ge(z_done, p + 1)
                        V.tensor_scalar(m.zh[:], psZ, 1 / A_SCALE, None, ALU.mult).then_inc(zh_ready, 1)
                        dve.wait_ge(zh_ready, p + 1)
                        V.scalar_tensor_tensor(m.zl[:], psZ, 1 / A_SCALE, m.zh[:], ALU.mult, ALU.subtract).then_inc(zl_ready, 1)
                        if not (last and u == 3):
                            low_turned(p + 1, u + 1)
                        if u == 0:
                            ids = load_ids(p + 2, 2 if last else U)
                        if not (last and u >= 2):
                            select(ids[4 * u:4 * u + 4], u)
                        dve.wait_ge(qt_done, p + 1)
                        for b in range(2):
                            rows, part = slice(32 * b, 32 * b + 32), slice(64 * b, 64 * b + 64)
                            V.tensor_copy(m.qt[rows, part], psQ[rows, part]).then_inc(qt_ready, 1)
                        dve.wait_ge(x1h_ready, p + 1)
                        V.tensor_tensor(m.x1l[:, u, :], m.xt[:, u, :], m.x1h[:, u, :], ALU.subtract).then_inc(x1l_ready, 1)
                        dve.wait_ge(qh_ready, p + 1)
                        V.tensor_tensor(m.ql[:, u % 2, :], psM[0:64, :], m.qh[0:64, u % 2, :], ALU.subtract).then_inc(ql_ready, 1)
                dve.wait_ge(cleared, 10)
                ids = load_ids(0, 2)
                for p in range(2):
                    select(ids[4 * p:4 * p + 4], p)
                low_turned(0, 0)
                turns(dve, body)

            @block.tensor
            def _(pe):
                def turn(p, u, count):
                    pe.wait_ge(x1_loaded[u % U], count)
                    for j in range(J):
                        last = PE.transpose(psT[:, j, :], m.xt[:, u % U, j * P:(j + 1) * P], ident[:])
                    last.then_inc(turned_done, 1)

                def mix(p, u, bank, early):
                    if bank == 0:
                        pe.wait_ge(x1l_ready, p + 1)
                        if not early:
                            pe.wait_ge(out_ready, p - 1)
                    o = ps[:, 2 + 2 * (u % 2) + bank, :]
                    cut = slice(bank * 512, bank * 512 + 512)
                    for k, (w, xp) in enumerate(((m.iwh, m.x1h), (m.iwh, m.x1l), (m.iwl, m.x1h))):
                        PE.matmul(o, w[:, bass.ds(p, 1), :].rearrange("p o d -> p (o d)"), xp[:, u, cut], start=(k == 0), stop=False)

                def turn_q(p, u):
                    pe.wait_ge(qt_ready, 2 * p + 2)
                    pe.wait_ge(m_selected, 2 * p + 2)
                    PE.matmul(psM, m.mp[:, u % 2, :, :].rearrange("p c n -> p (c n)"), m.qt[:], start=True, stop=True).then_inc(mq_done, 1)

                def add_adapters(p, u, count):
                    pe.wait_ge(ql_ready, p + 1)
                    pe.wait_ge(a_gathered[u], count)
                    for bank in range(2):
                        o = ps[:, 2 + 2 * (u % 2) + bank, :]
                        cut = slice(bank * 512, bank * 512 + 512)
                        PE.matmul(o, m.qh[:, u % 2, :], m.asel[:, u, cut], start=False, stop=False)
                        last = PE.matmul(o, m.ql[:, u % 2, :], m.asel[0:64, u, cut], start=False, stop=True)
                    last.then_inc(o_done, 1)

                def body(i, first, last):
                    for u in range(U):
                        p = i * U + u
                        has_prev = not (first and u == 0)
                        pu = (u - 1) % U
                        pe.wait_ge(x1Tl_ready, p + 1)
                        if not (last and u == 3):
                            turn(p + 1, u + 1, 16 * (i + 1 + (u + 1) // U))
                        if has_prev:
                            turn_q(p - 1, pu)
                        pe.wait_ge(b_selected, 4 * p + 4)
                        for j in range(J):
                            for k, (xT, b) in enumerate(((m.xTh, 0), (m.xTh, 1), (m.xTl, 0))):
                                done = PE.matmul(psZ, xT[:, u % 2, j, :], m.bsel[:, u % 2, :, b, j, :],
                                                 start=(j == 0 and k == 0), stop=(j == J - 1 and k == 2))
                        done.then_inc(z_done, 1)
                        if has_prev:
                            mix(p - 1, pu, 0, first and u < 3)
                            mix(p - 1, pu, 1, False)
                        pe.wait_ge(zl_ready, p + 1)
                        if has_prev:
                            pe.wait_ge(ql_ready, p)
                        for k, (z, w) in enumerate(((m.zh, m.iwh), (m.zh, m.iwl), (m.zl, m.iwh))):
                            done = PE.matmul(psQ, z[:], w[:, bass.ds(p, 1), :].rearrange("p o d -> p (o d)"), start=(k == 0), stop=(k == 2))
                        done.then_inc(qt_done, 1)
                        if has_prev:
                            add_adapters(p - 1, pu, 16 * (i + 1) if u else 16 * i)

                turn(0, 0, 16)
                turns(pe, body)
                turn_q(Q - 1, 3)
                mix(Q - 1, 3, 0, False)
                mix(Q - 1, 3, 1, False)
                add_adapters(Q - 1, 3, 16 * TURNS)


def program(nc, x, lens, id1, id2, id3, log_dt, C, log_A_real, A_imag, D, A1, B1, A2, B2, W, bias, out):
    with ExitStack() as ctx:
        m = storage(nc, ctx)
        setup_stage(nc, m, x, lens, id1, id2, id3, log_dt, C, log_A_real, A_imag, D, A1, B1, bias)
        channel_stage(nc, m, x, W, A2, B2)
        pair_stage(nc, m, out)


_INS = ['x', 'itok_B_8_3872', 'itok_B_3_7', 'itok_B_4_50', 'itok_B_0_31', 'L0_cond_log_dt', 'L0_cond_C', 'L0_cond_log_A_real',
        'L0_cond_A_imag', 'L0_cond_D', 'L1_cond_A', 'L1_cond_B', 'L2_cond_A', 'L2_cond_B', 'L3_cond_weights', 'L3_cond_biases']


def kernel(**inputs):
    import numpy as _np
    import concourse.bacc as _bacc
    from concourse import mybir as _mybir
    from concourse.bass_utils import run_bass_kernel_spmd as _run

    nc = _bacc.Bacc("TRN2", target_bir_lowering=False, num_devices=1)
    arrays, args = {}, []
    for name in _INS:
        a = _np.ascontiguousarray(inputs[name])
        arrays[f"in_{name}"] = a
        args.append(nc.dram_tensor(f"in_{name}", a.shape, _mybir.dt.from_np(a.dtype), kind="ExternalInput").ap())
    args.append(nc.dram_tensor("out_dram", inputs["x"].shape, F32, kind="ExternalOutput").ap())
    program(nc, *args)
    r = _run(nc, [arrays], core_ids=[0])
    return r.results[0]["out_dram"]
```

```python
from contextlib import ExitStack


import concourse.bass as bass
from concourse import mybir

F32 = mybir.dt.float32
F16 = mybir.dt.float16
I32 = mybir.dt.int32
U8 = mybir.dt.uint8
ALU = mybir.AluOpType
ACT = mybir.ActivationFunctionType

P = 128
B = 128
H = 64
L = 1024
J = L // P
N = 64
R = 16
N1, N2, NS = 8, 64, 32
Q = B // 2
G = 1 + N2 * R // P
TC = 32
KPAD = L + P
HALF, QUARTER = L // 2, L // 4
TW, DW = L - QUARTER, QUARTER + P
CH = H // 2
A_SCALE = 64.0
GROW = N1 * R * N2
U = 4

MAGIC = 12582912.0
LOG2E = 1.4426950408889634
LN2_HI, LN2_LO = 0.693359375, -2.12194440e-4
TURN = 6.2831853071795865
TWO_PI = 6.283185
PI_2 = 1.5707963267948966


class Storage:
    pass


def storage(nc, ctx):
    m = Storage()

    def sb(name, shape, dt):
        return ctx.enter_context(nc.sbuf_tensor(name, shape, dt))

    m.k_rows = nc.dram_tensor("k_rows", (H, 2, KPAD), F16).ap()
    m.d_rows = nc.dram_tensor("d_rows", (H, 2, L), F16).ap()
    m.x1_rows = nc.dram_tensor("x1_rows", (B, H, L), F32).ap()
    m.a_rows = nc.dram_tensor("a_rows", (2 * (N1 + N2) * R, L), F16).ap()
    m.g_rows = nc.dram_tensor("g_rows", (GROW + R, R), F32).ap()

    m.xt = sb("xt", [P, U, L], F32)
    m.toep = sb("toep", [P, U, 2, TW], F16)
    m.diff = sb("diff", [P, U, 2, 2, DW], F16)
    m.common = sb("common", [P, QUARTER], F32)
    m.xS = sb("xS", [P, 2, 2, P], F32)
    m.xSh = sb("xSh", [P, 2, 2, P], F16)
    m.xSl = sb("xSl", [P, 2, 2, P], F16)
    m.xTh = sb("xTh", [P, 2, J, P], F16)
    m.xTl = sb("xTl", [P, 2, J, P], F16)
    m.bt = sb("bt", [P, N1 + N2, 2, J, R], F16)
    m.iwh = sb("iwh", [P, Q, P], F16)
    m.iwl = sb("iwl", [P, Q, P], F16)
    m.g_pairs = sb("g_pairs", [64, Q, 2, R], F32)
    m.own = sb("own", [P, 2, H], F32)
    m.own_g = sb("own_g", [64, 2, R], F32)
    m.mask = sb("mask", [P, L], U8)
    m.ident = sb("ident", [P, P], F32)
    m.eye2 = sb("eye2", [P, H], F32)
    m.x1h = sb("x1h", [P, U, L], F16)
    m.x1l = sb("x1l", [P, U, L], F16)
    m.bsel = sb("bsel", [P, 2, 4, 2, J, R], F16)
    m.asel = sb("asel", [P, U, L], F16)
    m.outt = sb("outt", [P, 2, L], F32)
    m.ids = sb("ids", [P, 4, B], I32)
    m.sel_ids = sb("sel_ids", [1, Q, 2, 2], I32)
    m.idx_a = sb("idx_a", [P, Q], I32)
    m.idx_g = sb("idx_g", [P, Q], I32)
    m.idx_w = sb("idx_w", [P, Q], I32)
    m.idx_now = sb("idx_now", [P, U, 2], I32)
    m.bias_t = sb("bias_t", [P, Q], F32)
    m.zh = sb("zh", [P, 64], F16)
    m.zl = sb("zl", [P, 64], F16)
    m.qt = sb("qt", [64, P], F32)
    m.mp = sb("mp", [64, 2, 2, 64], F32)
    m.qh = sb("qh", [P, 2, P], F16)
    m.ql = sb("ql", [64, 2, P], F16)
    m.wnow = sb("wnow", [P, U, H], F32)
    m.wboth = sb("wboth", [P, 2, P], F32)
    m.gnow = sb("gnow", [64, U, R], F32)
    m.idf = sb("idf", [P, 4, B], F32)
    m.colf = sb("colf", [P, 4], F32)
    m.khl = sb("khl", [P, 2, CH * TC], F16)
    m.ps = ctx.enter_context(nc.psum_tensor("ps", [P, 8, 512], F32))

    def sem(name):
        return ctx.enter_context(nc.semaphore(name))

    m.x_loaded = [sem(f"x_loaded{u}") for u in range(U)]
    m.toep_loaded = [sem(f"toep_loaded{u}") for u in range(U)]
    m.k_rest_stored = sem("k_rest_stored")
    m.x1_loaded = [sem(f"x1_loaded{u}") for u in range(U)]
    m.a_stored = sem("a_stored")
    m.g_stored = sem("g_stored")
    m.xT_done, m.second_copied, m.xTh_ready = sem("xT_done"), sem("second_copied"), sem("xTh_ready")
    m.xTl_ready, m.xS_step, m.xS_ready = sem("xTl_ready"), sem("xS_step"), sem("xS_ready")
    m.turned = m.ps[:, 0:2, :].rearrange("p s (j n) -> p (s j) n", n=P)
    return m


def natural_b(m):
    return m.bsel[:].rearrange("p a b c d e -> p (a b c d e)").bitcast(F32)


def transposed_a(m):
    return m.asel[:, 0:2, :], m.asel[:, 2:4, :].rearrange("p s (j n) -> p s j n", j=J)


def by_adapter(turned):
    return turned.rearrange("p j (a r) -> p a j r", r=R)


def group_rows(m):
    return m.a_rows.rearrange("(s n) t -> n s t", s=2)


def load_toeplitz(m, sp, h, u):
    row = h * (2 * KPAD)
    sp.dma_start(m.toep[:, u, :, :], bass.AP(m.k_rows.tensor, row + QUARTER, [[1, P], [KPAD, 2], [1, TW]])).then_inc(m.toep_loaded[u], 16)
    sp.dma_start(m.diff[:, u, :, :, :],
                 bass.AP(m.d_rows.tensor, h * (2 * L), [[1, P], [HALF, 4], [1, DW]])).then_inc(m.toep_loaded[u], 16)


def turn_x(nc, m, u):
    for j in range(J):
        last = nc.tensor.transpose(m.turned[:, j, :], m.xt[:, u % U, j * P:(j + 1) * P], m.ident[:])
    last.then_inc(m.xT_done, 1)


def high_x(nc, m, u):
    nc.scalar.activation(m.xS[:, u % 2, :, :], m.turned[:, 2:4, :], ACT.Copy).then_inc(m.second_copied, 1)
    nc.scalar.activation(m.xTh[:, u % 2, :, :], m.turned, ACT.Copy).then_inc(m.xTh_ready, 1)


def low_x(nc, m, dve, h, u):
    V = nc.vector
    dve.wait_ge(m.xTh_ready, h + 1)
    V.tensor_tensor(m.xTl[:, u % 2, :, :], m.turned, m.xTh[:, u % 2, :, :], ALU.subtract).then_inc(m.xTl_ready, 1)
    both, high = m.xS[:, u % 2, :, :], m.xSh[:, u % 2, :, :]
    dve.wait_ge(m.second_copied, h + 1)
    V.tensor_tensor(both, m.turned[:, 0:2, :], both, ALU.add).then_inc(m.xS_step, 1)
    dve.wait_ge(m.xS_step, 2 * h + 1)
    V.tensor_copy(high, both).then_inc(m.xS_step, 1)
    dve.wait_ge(m.xS_step, 2 * h + 2)
    V.tensor_tensor(m.xSl[:, u % 2, :, :], both, high, ALU.subtract).then_inc(m.xS_ready, 1)


def load_x1(m, sp, p, u):
    sp.dma_start(m.xt[:, u, :], m.x1_rows.rearrange("b c t -> (b c) t")[bass.ds(p * P, P), :]).then_inc(m.x1_loaded[u], 16)


def setup_stage(nc, m, x, lens, id1, id2, id3, log_dt, C, log_A_real, A_imag, D, A1, B1, bias):
    ps, ident = m.ps, m.ident
    V, S, PE = nc.vector, nc.scalar, nc.tensor
    with ExitStack() as ctx:
        def sb(name, shape, dt):
            return ctx.enter_context(nc.sbuf_tensor(name, shape, dt))

        def sem(name):
            return ctx.enter_context(nc.semaphore(name))

        logs = sb("logs", [H, 72], F32)
        aim = sb("aim", [H, N], F32)
        cri = sb("cri", [H, N, 2], F32)
        work = sb("work", [H, 19, 72], F32)
        pow2 = sb("pow2", [H, 72], I32)
        packed = sb("packed", [H, 4, P], F32)
        par = sb("par", [P, 4, H], F32)
        step = sb("step", [P, 2, TC], F32)
        k0add = sb("k0add", [P, CH], F32)
        khl = m.khl
        zeros = sb("zeros", [P, P], F16)
        biases = sb("biases", [NS, H], F32)
        onehot = sb("onehot", [NS, B], F32)
        idf = m.idf
        lenc = sb("lenc", [P, 1], I32)
        lenf = sb("lenf", [P, 1], F32)
        coli = sb("coli", [P, 4], I32)
        colf = m.colf
        cols = sb("cols", [P, 12], F32)

        def halves(t):
            f = t.rearrange("p a b -> p (a b)").bitcast(F32)
            return f[:, 0:H * TC], f[:, H * TC:2 * H * TC]

        turns_v, turns_u = halves(m.iwh[:])
        decay_v, decay_u = halves(m.iwl[:])
        sin_u = m.x1h[:].rearrange("p a b -> p (a b)").bitcast(F32)
        cos_u = m.x1l[:].rearrange("p a b -> p (a b)").bitcast(F32)
        rounded_v = m.bt[:, N1:N1 + 16, :, :, :].rearrange("p a s j r -> p (a s j r)").bitcast(F32)
        a1f = m.outt[:, 0, :]
        iota_t = m.outt[:, 1, :]
        iota_i = m.bsel[:].rearrange("p a b c d e -> p (a b c d e)").bitcast(I32)
        nat_b = natural_b(m)
        spare = m.toep[:].rearrange("p u a b -> p (u a b)").bitcast(F32)
        nat_a, by_k = (spare[:, n * 1024:(n + 1) * 1024] for n in range(2))
        u_all = m.bt[:, N1 + 16:N1 + 48, :, :, :].rearrange("p a s j r -> p (a s j r)").bitcast(F32).rearrange("p (h n) -> p h n", h=H)
        at, a1c = transposed_a(m)

        def over_h(t):
            return t.rearrange("p (h c) -> p h c", c=TC)

        k_out = ps[:, 6:8, :].rearrange("p s n -> p (s n)")

        def blocks(k):
            return ps[:, k:k + 2, :].rearrange("p s (j n) -> p (s j) n", n=P)

        logs_loaded, aim_loaded, c_loaded, d_loaded = (sem(n) for n in ("logs_loaded", "aim_loaded", "c_loaded", "d_loaded"))
        ids_loaded = sem("ids_loaded")
        bias_loaded = sem("bias_loaded")
        const_made = sem("const_made")
        k0_cleared = sem("k0_cleared")
        iota_made = sem("iota_made")
        dve_step = sem("dve_step")
        angle_ready = sem("angle_ready")
        sine_ready = sem("sine_ready")
        packed_ready = sem("packed_ready")
        packed_turned = sem("packed_turned")
        par_ready = sem("par_ready")
        products = sem("products")
        decays = sem("decays")
        turns_v_ready, turns_u_ready = sem("turns_v_ready"), sem("turns_u_ready")
        v_ready = sem("v_ready")
        abs_u_ready = sem("abs_u_ready")
        trig_v, trig_s, trig_c = sem("trig_v"), sem("trig_s"), sem("trig_c")
        uv_ready = sem("uv_ready")
        k_done = sem("k_done")
        k_ready, k_high, khl_ready = sem("k_ready"), sem("k_high"), sem("khl_ready")
        k_stored = sem("k_stored")
        onehot_ready, bias_done = sem("onehot_ready"), sem("bias_done")
        b_loaded, a_loaded = sem("b_loaded"), sem("a_loaded")
        a_ordered = sem("a_ordered")
        b_turned, a_turned = sem("b_turned"), sem("a_turned")
        b_high, b_low, a_high, a_low = sem("b_high"), sem("b_low"), sem("a_high"), sem("a_low")
        a1_copied, a1_back, a1_high, a1_low = sem("a1_copied"), sem("a1_back"), sem("a1_high"), sem("a1_low")
        with nc.Block() as block:
            @block.sync
            def _(sp):
                sp.dma_start(logs[:, 0:64], log_A_real).then_inc(logs_loaded, 16)
                sp.dma_start(logs[:, 64:65], log_dt.rearrange("(h o) -> h o", o=1)).then_inc(logs_loaded, 16)
                sp.dma_start(aim[:], A_imag).then_inc(aim_loaded, 16)
                sp.dma_start(cri[:], C).then_inc(c_loaded, 16)
                sp.dma_start(nat_a.rearrange("p (a n) -> p a n", a=8), A1.rearrange("a (p k) r -> p a (k r)", k=J)).then_inc(a_loaded, 16)
                sp.wait_ge(iota_made, 2)
                sp.dma_start(nat_b, B1.rearrange("a r t -> (a r) t")).then_inc(b_loaded, 16)
                sp.wait_ge(k0_cleared, 1)
                sp.dma_start(k0add[TC - 1:P:2 * TC, :], D.rearrange("(q j) -> q j", j=CH)).then_inc(d_loaded, 16)
                sp.dma_start(lenc[:], lens.rearrange("(b o) -> b o", o=1)).then_inc(ids_loaded, 16)
                for n, v in enumerate((lens, id1, id2, id3)):
                    sp.dma_start(m.ids[:, n, :], v.rearrange("(o b) -> o b", o=1).broadcast_to([P, B])).then_inc(ids_loaded, 16)
                sp.dma_start(biases[:], bias.rearrange("s o d -> s (o d)")).then_inc(bias_loaded, 16)
                for h in range(3):
                    sp.dma_start(m.xt[:, h, :], x[:, h, :]).then_inc(m.x_loaded[h], 16)
                sp.wait_ge(const_made, 4)
                sp.dma_start(m.k_rows[:, :, L:KPAD].rearrange("h s z -> (h s) z"), zeros[:]).then_inc(k_stored, 16)
                sp.dma_start(m.g_rows[GROW:GROW + R, :], ident[0:R, 0:R]).then_inc(m.g_stored, 16)
                def store_k(q, signal):
                    for n, rows in enumerate((m.k_rows, m.d_rows)):
                        for part in range(2):
                            sp.dma_start(
                                rows[CH * q:CH * (q + 1), part, 0:L].rearrange("h (a c) -> a h c", c=TC),
                                khl[64 * q + 32 * n:64 * q + 32 * n + 32, part, :].rearrange("a (h c) -> a h c", c=TC)).then_inc(signal, 16)

                sp.wait_ge(khl_ready, 1)
                store_k(0, k_stored)
                sp.wait_ge(k_stored, 80)
                sp.wait_ge(a_turned, 1)
                for h in range(3):
                    load_toeplitz(m, sp, h, h)
                sp.wait_ge(a_low, 1)
                sp.dma_start(group_rows(m)[0:P, :, :], at).then_inc(m.a_stored, 16)
                sp.wait_ge(khl_ready, 2)
                store_k(1, m.k_rest_stored)

            @block.gpsimd
            def _(gp):
                gp.memset(k0add[:], 0.0).then_inc(k0_cleared, 1)
                gp.memset(ident[:], 0.0).then_inc(const_made, 1)
                gp.wait_ge(const_made, 1)
                gp.affine_select(out=ident[:], in_=ident[:], compare_op=ALU.not_equal, fill=1.0, base=0,
                                 pattern=[[-1, P]], channel_multiplier=1).then_inc(const_made, 1)
                gp.iota(iota_i, pattern=[[1, L]], base=0, channel_multiplier=0).then_inc(iota_made, 1)
                gp.iota(coli[:, 0:1], pattern=[[0, 1]], base=0, channel_multiplier=1).then_inc(const_made, 1)
                gp.memset(zeros[:], 0.0).then_inc(const_made, 1)
                gp.wait_ge(a_loaded, 16)
                gp.tensor_copy(by_k.rearrange("p (k a r) -> p k a r", k=J, a=8),
                               nat_a.rearrange("p (a k r) -> p k a r", a=8, k=J)).then_inc(a_ordered, 1)
                gp.wait_ge(par_ready, 1)
                for dst, s in ((decay_v, 0), (decay_u, 1)):
                    gp.tensor_tensor(over_h(dst), par[:, 0, :].unsqueeze(2).broadcast_to([P, H, TC]),
                                     step[:, s, :].unsqueeze(1).broadcast_to([P, H, TC]), ALU.mult).then_inc(products, 1)
                gp.wait_ge(trig_v, 1)
                gp.wait_ge(decays, 1)
                gp.tensor_tensor(turns_v, turns_v, decay_v, ALU.mult).then_inc(v_ready, 1)

            @block.scalar
            def _(act):
                act.wait_ge(angle_ready, 1)
                S.activation(work[:, 10, 0:64], work[:, 9, 0:64], ACT.Sin, scale=TWO_PI).then_inc(sine_ready, 1)
                S.activation(work[:, 11, 0:64], work[:, 9, 0:64], ACT.Sin, scale=TWO_PI / 2).then_inc(sine_ready, 1)
                act.wait_ge(b_turned, 1)
                S.activation(m.bt[:, 0:N1, 0, :, :], by_adapter(blocks(2)), ACT.Copy).then_inc(b_high, 1)
                act.wait_ge(a_turned, 1)
                S.activation(at[:, 0, :].rearrange("p (t k) -> p t k", k=J),
                             blocks(4).rearrange("p k t -> p t k"), ACT.Copy, scale=A_SCALE).then_inc(a_high, 1)
                act.wait_ge(m.xT_done, 1)
                high_x(nc, m, 0)
                act.wait_ge(products, 1)
                S.activation(decay_v, decay_v, ACT.Exp).then_inc(decays, 1)
                act.wait_ge(turns_u_ready, 1)
                S.activation(cos_u, turns_u, ACT.Abs).then_inc(abs_u_ready, 1)
                act.wait_ge(products, 2)
                S.activation(decay_u, decay_u, ACT.Exp).then_inc(decays, 1)
                S.activation(sin_u, turns_u, ACT.Sin, scale=-TWO_PI).then_inc(trig_s, 1)
                act.wait_ge(abs_u_ready, 1)
                S.activation(cos_u, cos_u, ACT.Sin, scale=-TWO_PI, bias=cols[:, 2:3]).then_inc(trig_c, 1)
                act.wait_ge(turns_v_ready, 1)
                S.activation(turns_v, turns_v, ACT.Sin, scale=-TWO_PI, bias=cols[:, 1:2]).then_inc(trig_v, 1)
                for q in range(2):
                    rows = slice(64 * q, 64 * q + 64)
                    act.wait_ge(k_ready, q + 1)
                    S.activation(khl[rows, 0, :], k_out[rows, :], ACT.Copy).then_inc(k_high, 1)
                act.wait_ge(a1_back, 1)
                S.activation(a1c[:, 0, :, :], blocks(2), ACT.Copy, scale=A_SCALE).then_inc(a1_high, 1)

            @block.tensor
            def _(pe):
                pe.wait_ge(const_made, 2)
                pe.wait_ge(b_loaded, 16)
                for j in range(J):
                    last = PE.transpose(blocks(2)[:, j, :], nat_b[:, j * P:(j + 1) * P], ident[:])
                last.then_inc(b_turned, 1)
                pe.wait_ge(a_ordered, 1)
                for k in range(J):
                    last = PE.transpose(blocks(4)[:, k, :], by_k[:, k * P:(k + 1) * P], ident[:])
                last.then_inc(a_turned, 1)
                pe.wait_ge(packed_ready, 1)
                for n in range(4):
                    last = PE.transpose(ps[:, 7, n * H:(n + 1) * H], packed[:, n, :], ident[0:H, 0:H])
                last.then_inc(packed_turned, 1)
                pe.wait_ge(m.x_loaded[0], 16)
                turn_x(nc, m, 0)
                pe.wait_ge(v_ready, 1)
                for h in range(H):
                    q, j = h // CH, h % CH
                    if j == 0:
                        pe.wait_ge(uv_ready, q + 1)
                    last = PE.matmul(k_out[64 * q:64 * q + 64, j * TC:(j + 1) * TC], u_all[:, h, :],
                                     over_h(turns_v)[:, h, :], start=True, stop=True)
                    if j == CH - 1:
                        last.then_inc(k_done, 1)
                pe.wait_ge(a1_copied, 1)
                pe.wait_ge(b_low, 1)
                for j in range(J):
                    last = PE.transpose(blocks(2)[:, j, :], a1f[:, j * P:(j + 1) * P], ident[:])
                last.then_inc(a1_back, 1)
                pe.wait_ge(bias_loaded, 16)
                pe.wait_ge(onehot_ready, 1)
                pe.wait_ge(a_low, 1)
                for b in range(2):
                    last = PE.matmul(ps[64 * b:64 * b + 64, 4, 0:Q], biases[:],
                                     onehot[:].rearrange("s (q b) -> s b q", b=2)[:, b, :], start=True, stop=True)
                last.then_inc(bias_done, 1)

            @block.vector
            def _(dve):
                steps = [0]

                def step_of(ins):
                    ins.then_inc(dve_step, 1)
                    steps[0] += 1

                def settle():
                    dve.wait_ge(dve_step, steps[0])

                def link(ins):
                    step_of(ins)
                    settle()

                def t(n, w=64):
                    return work[:, n, 0:w]

                def exp_parts(src, w):
                    k, r, e = t(0, w), t(1, w), t(2, w)
                    link(V.tensor_scalar(k, src, LOG2E, MAGIC, ALU.mult, ALU.add))
                    link(V.tensor_scalar(k, k, MAGIC, -126.0, ALU.subtract, ALU.max))
                    step_of(V.tensor_scalar(pow2[:, 0:w], k, 127.0, 8388608.0, ALU.add, ALU.mult))
                    link(V.scalar_tensor_tensor(r, k, -LN2_HI, src, ALU.mult, ALU.add))
                    step_of(V.tensor_copy(t(3, w), pow2[:, 0:w].bitcast(F32)))
                    link(V.scalar_tensor_tensor(r, k, -LN2_LO, r, ALU.mult, ALU.add))
                    link(V.tensor_scalar(e, r, 1 / 5040, None, ALU.mult))
                    for c in (1 / 720, 1 / 120, 1 / 24, 1 / 6, 1 / 2, 1.0):
                        link(V.scalar_tensor_tensor(e, e, c, r, ALU.add, ALU.mult))

                dve.wait_ge(iota_made, 1)
                V.tensor_copy(iota_t, iota_i).then_inc(iota_made, 1)
                dve.wait_ge(iota_made, 2)
                step_of(V.memset(cols[0:64, 1:2], PI_2))
                step_of(V.memset(cols[64:128, 1:2], 0.0))
                step_of(V.memset(cols[:, 2:3], PI_2))
                step_of(V.tensor_scalar(step[:, 0, :], iota_t[:, 0:TC], -1.0, TC - 1.0, ALU.mult, ALU.add))

                dve.wait_ge(logs_loaded, 32)
                exp_parts(logs[:, 0:65], 65)
                link(V.scalar_tensor_tensor(t(4, 65), t(2, 65), 1.0, t(3, 65), ALU.add, ALU.mult))
                nar, dt = t(4), work[:, 4, 64:65]
                dve.wait_ge(aim_loaded, 16)
                step_of(V.tensor_scalar(t(6), aim[:], dt, 1 / TURN, ALU.mult, ALU.mult))
                step_of(V.tensor_scalar(t(5), nar, dt, -1.0, ALU.mult, ALU.mult))
                step_of(V.tensor_tensor(t(17), nar, nar, ALU.mult))
                step_of(V.tensor_tensor(t(18), aim[:], aim[:], ALU.mult))
                link(V.tensor_scalar(step[:, 1, :], step[:, 0, :], float(TC), None, ALU.mult))
                step_of(V.tensor_scalar(t(7), t(6), MAGIC, None, ALU.add))
                link(V.tensor_tensor(t(17), t(17), t(18), ALU.add))
                step_of(V.tensor_scalar(t(8), t(7), MAGIC, None, ALU.subtract))
                link(V.reciprocal(t(17), t(17)))
                V.tensor_tensor(t(9), t(6), t(8), ALU.subtract).then_inc(angle_ready, 1)
                for half in (slice(0, 64), slice(64, 128)):
                    step_of(V.tensor_copy(packed[:, 0, half], t(5)))
                    step_of(V.tensor_copy(packed[:, 1, half], t(6)))
                exp_parts(t(5), 64)
                link(V.tensor_tensor(t(0), t(2), t(3), ALU.mult))
                link(V.scalar_tensor_tensor(t(1), t(3), -1.0, t(0), ALU.add, ALU.add))
                dve.wait_ge(sine_ready, 2)
                step_of(V.tensor_tensor(t(8), t(11), t(11), ALU.mult))
                link(V.tensor_scalar(t(2), t(1), 1.0, None, ALU.add))
                step_of(V.tensor_tensor(t(7), t(2), t(10), ALU.mult))
                link(V.tensor_tensor(t(8), t(8), t(2), ALU.mult))
                step_of(V.tensor_tensor(t(3), t(7), aim[:], ALU.mult))
                step_of(V.tensor_tensor(t(15), t(7), nar, ALU.mult))
                link(V.scalar_tensor_tensor(t(12), t(8), -2.0, t(1), ALU.mult, ALU.add))
                step_of(V.tensor_tensor(t(2), t(12), nar, ALU.mult))
                link(V.tensor_tensor(t(16), t(12), aim[:], ALU.mult))
                step_of(V.tensor_tensor(t(13), t(3), t(2), ALU.subtract))
                link(V.tensor_tensor(t(14), t(15), t(16), ALU.add))
                step_of(V.scalar_tensor_tensor(t(13), t(13), 2.0, t(17), ALU.mult, ALU.mult))
                link(V.scalar_tensor_tensor(t(14), t(14), -2.0, t(17), ALU.mult, ALU.mult))
                dve.wait_ge(c_loaded, 16)
                cr, ci = cri[:, :, 0], cri[:, :, 1]
                step_of(V.tensor_tensor(t(0), cr, t(13), ALU.mult))
                step_of(V.tensor_tensor(t(1), ci, t(14), ALU.mult))
                step_of(V.tensor_tensor(t(2), cr, t(14), ALU.mult))
                link(V.tensor_tensor(t(3), ci, t(13), ALU.mult))
                step_of(V.tensor_tensor(packed[:, 2, 0:64], t(0), t(1), ALU.subtract))
                step_of(V.scalar_tensor_tensor(packed[:, 2, 64:128], t(2), -1.0, t(3), ALU.mult, ALU.subtract))
                step_of(V.tensor_tensor(packed[:, 3, 0:64], t(2), t(3), ALU.add))
                link(V.tensor_tensor(packed[:, 3, 64:128], t(0), t(1), ALU.subtract))
                dve.sem_inc(packed_ready, 1)
                dve.wait_ge(packed_turned, 1)
                V.tensor_copy(par[:], ps[:, 7, 0:4 * H].rearrange("p (n h) -> p n h", n=4)).then_inc(par_ready, 1)
                dve.wait_ge(par_ready, 1)

                def product(dst, s):
                    link(V.tensor_tensor(over_h(dst), par[:, 1, :].unsqueeze(2).broadcast_to([P, H, TC]),
                                         step[:, s, :].unsqueeze(1).broadcast_to([P, H, TC]), ALU.mult))

                product(turns_u, 1)
                link(V.tensor_scalar(cos_u, turns_u, MAGIC, None, ALU.add))
                V.scalar_tensor_tensor(turns_u, cos_u, MAGIC, turns_u, ALU.subtract, ALU.subtract).then_inc(turns_u_ready, 1)
                product(turns_v, 0)
                link(V.tensor_scalar(rounded_v, turns_v, MAGIC, None, ALU.add))
                link(V.scalar_tensor_tensor(turns_v, rounded_v, MAGIC, turns_v, ALU.subtract, ALU.subtract))
                V.scalar_tensor_tensor(turns_v[0:64, :], turns_v[0:64, :], -1.0, turns_v[0:64, :], ALU.mult, ALU.max).then_inc(turns_v_ready, 1)
                dve.wait_ge(const_made, 3)
                link(V.tensor_scalar(coli[:, 1:2], coli[:, 0:1], 2 * TC - 1, None, ALU.bitwise_and))
                link(V.tensor_copy(cols[:, 10:11], coli[:, 1:2]))
                link(V.tensor_scalar(cols[:, 10:11], cols[:, 10:11], TC - 1.0, None, ALU.is_equal))
                dve.wait_ge(d_loaded, 16)
                link(V.tensor_scalar(k0add[:], k0add[:], cols[:, 10:11], None, ALU.add))
                dve.wait_ge(turns_v_ready, 1)
                for half in range(2):
                    hs = slice(half * H // 2, (half + 1) * H // 2)
                    cut = slice(half * H // 2 * TC, (half + 1) * H // 2 * TC)

                    def coefficient(n):
                        return par[:, n, hs].unsqueeze(2).broadcast_to([P, H // 2, TC])

                    if half == 0:
                        dve.wait_ge(trig_s, 1)
                    step_of(V.tensor_tensor(over_h(sin_u)[:, hs, :], over_h(sin_u)[:, hs, :], coefficient(3), ALU.mult))
                    if half == 0:
                        dve.wait_ge(trig_c, 1)
                    link(V.tensor_tensor(over_h(cos_u)[:, hs, :], over_h(cos_u)[:, hs, :], coefficient(2), ALU.mult))
                    link(V.tensor_tensor(cos_u[:, cut], cos_u[:, cut], sin_u[:, cut], ALU.subtract))
                    if half == 0:
                        dve.wait_ge(decays, 2)
                    link(V.tensor_tensor(u_all[:, hs, 0:TC], over_h(cos_u)[:, hs, :], over_h(decay_u)[:, hs, :], ALU.mult))
                    step_of(V.tensor_tensor(u_all[:, hs, 32:48], u_all[:, hs, 0:16], u_all[:, hs, 8:24], ALU.subtract))
                    link(V.tensor_tensor(u_all[:, hs, 48:64], u_all[:, hs, 16:32], u_all[:, hs, 8:24], ALU.subtract))
                    dve.sem_inc(uv_ready, 1)

                def complete_k(q):
                    rows = slice(64 * q, 64 * q + 64)
                    dve.wait_ge(k_done, q + 1)
                    k0 = over_h(k_out[rows, :])[:, :, TC - 1]
                    V.tensor_tensor(k0, k0, k0add[rows, :], ALU.add).then_inc(k_ready, 1)

                def k_low(q):
                    rows = slice(64 * q, 64 * q + 64)
                    dve.wait_ge(k_high, q + 1)
                    V.tensor_tensor(khl[rows, 1, :], k_out[rows, :], khl[rows, 0, :], ALU.subtract).then_inc(khl_ready, 1)

                complete_k(0)
                dve.wait_ge(b_high, 1)
                V.tensor_tensor(m.bt[:, 0:N1, 1, :, :], by_adapter(blocks(2)), m.bt[:, 0:N1, 0, :, :], ALU.subtract).then_inc(b_low, 1)
                k_low(0)
                dve.wait_ge(a_high, 1)
                turned = blocks(4).rearrange("p k t -> p t k")
                V.tensor_copy(a1f.rearrange("p (t k) -> p t k", k=J), turned).then_inc(a1_copied, 1)
                V.scalar_tensor_tensor(at[:, 1, :].rearrange("p (t k) -> p t k", k=J), turned, A_SCALE,
                                       at[:, 0, :].rearrange("p (t k) -> p t k", k=J), ALU.mult, ALU.subtract).then_inc(a_low, 1)
                complete_k(1)
                low_x(nc, m, dve, 0, 0)
                k_low(1)
                dve.wait_ge(a1_high, 1)
                V.scalar_tensor_tensor(a1c[:, 1, :, :], blocks(2), A_SCALE, a1c[:, 0, :, :], ALU.mult, ALU.subtract).then_inc(a1_low, 1)
                dve.wait_ge(ids_loaded, 80)
                step_of(V.tensor_copy(idf[:], m.ids[:]))
                step_of(V.tensor_copy(lenf[:], lenc[:]))
                step_of(V.tensor_scalar(coli[:, 1:2], coli[:, 0:1], 4, 1, ALU.logical_shift_right, ALU.bitwise_and))
                step_of(V.tensor_scalar(coli[:, 2:3], coli[:, 0:1], 15, None, ALU.bitwise_and))
                link(V.tensor_scalar(coli[:, 3:4], coli[:, 0:1], 6, None, ALU.logical_shift_right))
                step_of(V.tensor_scalar(m.mask[:], iota_t, lenf[:, 0:1], None, ALU.is_lt))
                link(V.tensor_copy(colf[:], coli[:]))
                V.tensor_scalar(onehot[:], idf[0:NS, 3, :], colf[0:NS, 0:1], None, ALU.is_equal).then_inc(onehot_ready, 1)

                dve.wait_ge(bias_done, 1)
                link(V.tensor_copy(m.bias_t[:], ps[:, 4, 0:Q]))
                dve.wait_ge(a1_low, 1)
                dve.wait_ge(b_low, 1)


def channel_stage(nc, m, x, W, A2, B2):
    ps, ident = m.ps, m.ident
    V, S, PE, GP = nc.vector, nc.scalar, nc.tensor, nc.gpsimd
    TURNS = H // U
    with ExitStack() as ctx:
        def sem(name):
            return ctx.enter_context(nc.semaphore(name))

        tmp = ctx.enter_context(nc.sbuf_tensor("tmp", [P, 2, Q], F32))
        cols = ctx.enter_context(nc.sbuf_tensor("row_cols", [P, 10], F32))
        row_step, rows_ready = sem("row_step"), sem("rows_ready")
        x1_stored = [sem(f"x1_stored{u}") for u in range(U)]
        low_done = sem("low_done")
        conv_done = sem("conv_done")
        common_added = sem("common_added")
        low_ready = sem("low_ready")
        x1_ready = sem("x1_ready")
        idx_copied = sem("idx_copied")
        held = sem("held")
        held_gather = sem("held_gather")
        w_gathered = [sem(f"w_gathered{u}") for u in range(U)]
        g_gathered = [sem(f"g_gathered{u}") for u in range(U)]
        w_both = sem("w_both")
        w_plus = sem("w_plus")
        w_high = sem("w_high")
        w_low = sem("w_low")
        g_kept = sem("g_kept")
        b_loaded, a_loaded, a_ordered = sem("b_loaded"), sem("a_loaded"), sem("a_ordered")
        b_turned, a_turned = sem("b_turned"), sem("a_turned")
        b_high, b_low, a_high, a_low = sem("b_high"), sem("b_low"), sem("a_high"), sem("a_low")
        g_done = sem("g_done")
        g_out_ready = sem("g_out_ready")

        nat_b = natural_b(m)
        nat_a = m.outt[:, 0, :]
        by_k = m.outt[:, 1, :]
        at, a1c = transposed_a(m)
        g_out = m.x1h[:, 0, 0:2 * P].bitcast(F32)

        conv_low = ps[:, 4, :]

        def conv_high(h2):
            return ps[:, 5 + h2, :]

        conv_common = ps[:, 7, 0:QUARTER]

        group_turned = ps[:, 2:4, :].rearrange("p s (j n) -> p (s j) n", n=P)
        group_g = ps[:, 2, 0:P]

        def turns(eng, body):
            body(0, first=True, next_group=True)
            with eng.Fori(1, G - 1) as i:
                body(i, group=True, next_group=True)
            body(G - 1, group=True)
            with eng.Fori(G, TURNS - 1) as i:
                body(i)
            body(TURNS - 1, last=True)

        with nc.Block() as block:
            @block.sync
            def _(sp):
                def load_x(h, u):
                    sp.dma_start(m.xt[:, u, :], x[:, bass.ds(h, 1), :].rearrange("b o t -> b (o t)")).then_inc(m.x_loaded[u], 16)

                def body(i, first=False, last=False, group=False, next_group=False):
                    for u in range(U):
                        h = i * U + u
                        if not (last and u):
                            v = (u + 3) % U
                            if not (first and u == 0):
                                sp.wait_ge(x1_stored[v], 16 * (i + (1 if u else 0)))
                            load_x(h + 3, v)
                            load_toeplitz(m, sp, h + 3, v)
                        if next_group and u == 2:
                            if group:
                                sp.wait_ge(b_turned, i)
                                sp.wait_ge(a_turned, i)
                            load_group(i + 1)
                    if first:
                        sp.wait_ge(m.k_rest_stored, 64)
                    if group:
                        sp.wait_ge(g_out_ready, i + 1)
                        rows = m.g_rows[0:GROW, :].rearrange("(n a) r -> n a r", n=P)
                        sp.dma_start(rows[:, bass.ds((i - 1) * 8, 8), :], g_out.rearrange("p (a r) -> p a r", r=R)).then_inc(m.g_stored, 16)
                        sp.dma_start(group_rows(m)[bass.ds(i * P, P), :, :], at).then_inc(m.a_stored, 16)

                def load_group(g):
                    sp.dma_start(nat_b, B2.rearrange("a r t -> (a r) t")[bass.ds((g - 1) * P, P), :]).then_inc(b_loaded, 16)
                    sp.dma_start(nat_a.rearrange("p (a n) -> p a n", a=8),
                                 A2.rearrange("a (p k) r -> p a (k r)", k=J)[:, bass.ds((g - 1) * 8, 8), :]).then_inc(a_loaded, 16)

                turns(sp, body)
                sp.wait_ge(m.a_stored, 16 * G)
                for u in range(U):
                    sp.wait_ge(x1_stored[u], 16 * (TURNS + (1 if u == 3 else 0)))
                for p in range(3):
                    load_x1(m, sp, p, p)

            @block.gpsimd
            def _(gp):
                w_src = W.rearrange("s c d -> (s c) d")

                def gather_w(q, v):
                    GP.tensor_copy(m.idx_now[:, v, 0:1], m.idx_w[:, bass.ds(q, 1)]).then_inc(idx_copied, 1)
                    gp.wait_ge(idx_copied, q + 1)
                    gp.sem_inc(held_gather, 1)
                    gp.indirect_dma_start(m.wnow[:, v, :], None, w_src,
                                          bass.IndirectOffsetOnAxis(ap=m.idx_now[:, v, 0:1], axis=0)).then_inc(w_gathered[v], 16)

                def keep_w(i, first=False, last=False):
                    for u in range(U):
                        q = i * U + u
                        if not (last and u):
                            if not (first and u == 0):
                                gp.wait_ge(w_both, q)
                            gather_w(q + 3, (u + 3) % U)
                        gp.wait_ge(w_gathered[u], 16 * (i + 1))
                        GP.tensor_tensor(m.wnow[:, u, :], m.wnow[:, u, :], m.eye2[:], ALU.add).then_inc(w_plus, 1)
                        gp.wait_ge(w_plus, q + 1)
                        both = m.wboth[:, u % 2, :]
                        GP.tensor_tensor(both.rearrange("p (b d) -> p b d", b=2), m.wnow[:, u:u + 1, :].broadcast_to([P, 2, H]),
                                         m.own[:], ALU.mult).then_inc(w_both, 1)
                        gp.wait_ge(w_both, q + 1)
                        high = m.iwh[:, bass.ds(q, 1), :].rearrange("p o d -> p (o d)")
                        GP.tensor_copy(high, both).then_inc(w_high, 1)
                        gp.wait_ge(w_high, q + 1)
                        GP.tensor_tensor(m.iwl[:, bass.ds(q, 1), :].rearrange("p o d -> p (o d)"), both, high,
                                         ALU.subtract).then_inc(w_low, 1)

                def gather_g(q, v):
                    GP.tensor_copy(m.idx_now[:, v, 1:2], m.idx_g[:, bass.ds(q, 1)]).then_inc(idx_copied, 1)
                    gp.wait_ge(idx_copied, Q + q + 1)
                    gp.sem_inc(held_gather, 1)
                    gp.indirect_dma_start(m.gnow[:, v, :], None, m.g_rows,
                                          bass.IndirectOffsetOnAxis(ap=m.idx_now[0:64, v, 1:2], axis=0)).then_inc(g_gathered[v], 16)

                def keep_g(i, first=False, last=False):
                    for u in range(U):
                        q = i * U + u
                        if not (last and u):
                            if not (first and u == 0):
                                gp.wait_ge(g_kept, q)
                            gather_g(q + 3, (u + 3) % U)
                        gp.wait_ge(g_gathered[u], 16 * (i + 1))
                        GP.tensor_tensor(m.g_pairs[:, bass.ds(q, 1), :, :].rearrange("p o b r -> p (o b) r"),
                                         m.gnow[:, u:u + 1, :].broadcast_to([64, 2, R]), m.own_g[:], ALU.mult).then_inc(g_kept, 1)

                def all_pairs(gather, keep):
                    for q in range(3):
                        gather(q, q)
                    keep(0, first=True)
                    with gp.Fori(1, TURNS - 1) as i:
                        keep(i)
                    keep(TURNS - 1, last=True)

                gp.wait_ge(rows_ready, 1)
                all_pairs(gather_w, keep_w)
                gp.wait_ge(m.g_stored, 16 * G)
                all_pairs(gather_g, keep_g)
                gp.wait_ge(w_low, Q)
                gp.wait_ge(g_kept, Q)

            @block.scalar
            def _(act):
                def store_x1(h, u):
                    act.wait_ge(low_ready, h + 1)
                    act.wait_ge(x1_ready, h + 1)
                    act.dma_start(m.x1_rows[:, bass.ds(h, 1), :].rearrange("b o t -> b (o t)"), m.xt[:, u, :]).then_inc(x1_stored[u], 16)

                def body(i, first=False, last=False, group=False, next_group=False):
                    for u in range(U):
                        h = i * U + u
                        if not (first and u == 0):
                            act.wait_ge(m.xT_done, h + 1)
                            if not (first and u < 2):
                                act.wait_ge(conv_done, h - 1)
                            high_x(nc, m, u)
                        if not (first and u < 2):
                            store_x1(h - 2, (u - 2) % U)
                        if group and u == 0:
                            act.wait_ge(a_loaded, 16 * i)
                            S.activation(by_k.rearrange("p (k a r) -> p k a r", k=J, a=8),
                                         nat_a.rearrange("p (a k r) -> p k a r", a=8, k=J), ACT.Copy).then_inc(a_ordered, 1)
                        if group and u == 1:
                            act.wait_ge(b_turned, i)
                            S.activation(m.bt[:, bass.ds(i * 8, 8), 0, :, :], by_adapter(group_turned), ACT.Copy).then_inc(b_high, 1)
                        if group and u == 2:
                            act.wait_ge(a_turned, i)
                            act.wait_ge(m.a_stored, 16 * i)
                            S.activation(at[:, 0, :].rearrange("p (t k) -> p t k", k=J),
                                         group_turned.rearrange("p k t -> p t k"), ACT.Copy, scale=A_SCALE).then_inc(a_high, 1)
                        if group and u == 3:
                            act.wait_ge(g_done, i)
                            act.wait_ge(m.g_stored, 16 * i)
                            S.activation(g_out, group_g, ACT.Copy, scale=1 / A_SCALE).then_inc(g_out_ready, 1)

                act.sem_inc(g_out_ready, 1)
                turns(act, body)
                store_x1(H - 2, 2)
                for half, ready in enumerate((low_ready, x1_ready)):
                    act.wait_ge(ready, H)
                    cut = slice(half * HALF, (half + 1) * HALF)
                    act.dma_start(m.x1_rows[:, H - 1, cut], m.xt[:, 3, cut]).then_inc(x1_stored[3], 16)

            @block.vector
            def _(dve):
                def selection_rows():
                    steps = [0]

                    def step_of(ins):
                        ins.then_inc(row_step, 1)
                        steps[0] += 1

                    def settle():
                        dve.wait_ge(row_step, steps[0])

                    def link(ins):
                        step_of(ins)
                        settle()

                    pf, lf, rf, sf = (m.colf[:, n:n + 1] for n in range(4))

                    def col(n, rows=slice(0, P)):
                        return cols[rows, n:n + 1]

                    step_of(V.tensor_scalar(col(3), lf, -1.0, 1.0, ALU.mult, ALU.add))
                    step_of(V.tensor_scalar(col(5), lf, float(R), None, ALU.mult))
                    step_of(V.scalar_tensor_tensor(col(9), sf, -64.0, pf, ALU.mult, ALU.add))
                    link(V.scalar_tensor_tensor(col(6), sf, float((N1 + N2) * R), rf, ALU.mult, ALU.add))
                    step_of(V.tensor_scalar(col(4), col(3), float(R), None, ALU.mult))
                    step_of(V.scalar_tensor_tensor(col(6), lf, float(N1 * R), col(6), ALU.mult, ALU.add))
                    step_of(V.tensor_scalar(col(7), col(3), float(R * N2), None, ALU.mult))
                    link(V.scalar_tensor_tensor(col(8), col(3), float(N2), lf, ALU.mult, ALU.add))
                    link(V.tensor_tensor(col(8), col(8), rf, ALU.mult))
                    link(V.scalar_tensor_tensor(col(8), lf, float(GROW), col(8), ALU.mult, ALU.add))
                    pair = m.idf[:].rearrange("p n (q b) -> p n b q", b=2)
                    for k in range(4):
                        rows, b = slice(32 * k, 32 * k + 32), k % 2
                        step_of(V.tensor_scalar(tmp[rows, 0, :], pair[rows, 1, b, :], col(4, rows), col(6, rows), ALU.mult, ALU.add))
                        step_of(V.tensor_scalar(tmp[rows, 1, :], pair[rows, 1, b, :], col(7, rows), col(8, rows), ALU.mult, ALU.add))
                    settle()
                    for k in range(4):
                        rows, b = slice(32 * k, 32 * k + 32), k % 2
                        step_of(V.scalar_tensor_tensor(m.idx_a[rows, :], pair[rows, 2, b, :], col(5, rows), tmp[rows, 0, :], ALU.mult, ALU.add))
                        step_of(V.scalar_tensor_tensor(m.idx_g[rows, :], pair[rows, 2, b, :], col(3, rows), tmp[rows, 1, :], ALU.mult, ALU.add))
                    step_of(V.memset(m.own[:], 0.0))
                    step_of(V.memset(m.own_g[:], 0.0))
                    settle()
                    for b in range(2):
                        rows = slice(64 * b, 64 * b + 64)
                        step_of(V.tensor_scalar(m.idx_w[rows, :], pair[rows, 3, b, :], float(H), col(9, rows), ALU.mult, ALU.add))
                        step_of(V.tensor_copy(m.eye2[rows, :], ident[rows, 64 * b:64 * b + 64]))
                        step_of(V.memset(m.own[rows, b, :], 1.0))
                        step_of(V.memset(m.own_g[32 * b:32 * b + 32, b, :], 1.0))
                    for layer in range(2):
                        step_of(V.tensor_copy(m.sel_ids[:, :, :, layer], m.ids[0:1, 1 + layer, :].rearrange("o (q b) -> o q b", b=2)))
                    settle()
                    dve.sem_inc(rows_ready, 1)

                def body(i, first=False, last=False, group=False, next_group=False):
                    for u in range(U):
                        h = i * U + u
                        if not (last and u == 3):
                            low_x(nc, m, dve, h + 1, u + 1)
                        dve.wait_ge(low_done, h + 1)
                        dve.sem_inc(held, 1)
                        V.copy_predicated(m.xt[:, u, 0:HALF], m.mask[:, 0:HALF], conv_low[:, ::-1]).then_inc(low_ready, 1)
                        dve.wait_ge(conv_done, h + 1)
                        V.tensor_copy(m.common[:], conv_common).then_inc(common_added, 1)
                        dve.wait_ge(common_added, 2 * h + 1)
                        high = conv_high(u % 2)
                        V.tensor_tensor(high.rearrange("p (q n) -> p q n", q=2), high.rearrange("p (q n) -> p q n", q=2),
                                        m.common[:].unsqueeze(1).broadcast_to([P, 2, QUARTER]), ALU.add).then_inc(common_added, 1)
                        dve.wait_ge(common_added, 2 * h + 2)
                        dve.sem_inc(held, 1)
                        V.copy_predicated(m.xt[:, u, HALF:L], m.mask[:, HALF:L], high[:, ::-1]).then_inc(x1_ready, 1)
                        if group and u == 0:
                            dve.wait_ge(b_high, i)
                            cut = bass.ds(i * 8, 8)
                            V.tensor_tensor(m.bt[:, cut, 1, :, :], by_adapter(group_turned), m.bt[:, cut, 0, :, :], ALU.subtract).then_inc(b_low, 1)
                        if group and u == 1:
                            dve.wait_ge(a_high, i)
                            V.scalar_tensor_tensor(at[:, 1, :].rearrange("p (t k) -> p t k", k=J), group_turned.rearrange("p k t -> p t k"), A_SCALE,
                                                   at[:, 0, :].rearrange("p (t k) -> p t k", k=J), ALU.mult, ALU.subtract).then_inc(a_low, 1)

                selection_rows()
                turns(dve, body)

            @block.tensor
            def _(pe):
                def turn(i, u):
                    h = i * U + u
                    pe.wait_ge(m.x_loaded[u % U], 16 * (i + 1 + u // U))
                    pe.wait_ge(m.xS_ready, h)
                    turn_x(nc, m, u)

                def convolve(i, u, early):
                    h = i * U + u
                    toep, diff = m.toep[:, u, :, :], m.diff[:, u, :, :, :]

                    def products(out, xs, rhs, start, stop):
                        for k, (x_part, part) in enumerate(((0, 0), (0, 1), (1, 0))):
                            last = PE.matmul(out, xs[x_part], rhs(part), start=start and k == 0, stop=stop and k == 2)
                        return last

                    def blocks_of(parts, j):
                        return [t[:, u % 2, j, :] for t in parts]

                    x_parts, s_parts = (m.xTh, m.xTl), (m.xSh, m.xSl)
                    pe.wait_ge(m.xTl_ready, h + 1)
                    pe.wait_ge(m.toep_loaded[u], 32 * (i + 1))
                    if not (early and u == 0):
                        pe.wait_ge(low_ready, h)
                    for j in range(4):
                        last = products(conv_low[:, 0:HALF - j * P], blocks_of(x_parts, j),
                                        lambda part: toep[:, part, HALF - QUARTER + j * P:TW], j == 0, j == 3)
                    last.then_inc(low_done, 1)
                    if not early:
                        pe.wait_ge(x1_ready, h - 1)
                    high = conv_high(u % 2)
                    for j in range(4, J):
                        products(high[:, 0:L - j * P], blocks_of(x_parts, j),
                                 lambda part: toep[:, part, j * P - QUARTER:TW], j == 4, False)
                    for n in range(2):
                        for j in range(2):
                            products(high[:, n * QUARTER:(n + 1) * QUARTER], blocks_of(x_parts, 2 * n + j),
                                     lambda part: diff[:, part, n, j * P:j * P + QUARTER], False, n == 1 and j == 1)
                    pe.wait_ge(m.xS_ready, h + 1)
                    if not (early and u == 0):
                        pe.wait_ge(common_added, 2 * h - 1)
                    for j in range(2):
                        last = products(conv_common, blocks_of(s_parts, j),
                                        lambda part: toep[:, part, j * P:j * P + QUARTER], j == 0, j == 1)
                    last.then_inc(conv_done, 1)

                def turn_b(g):
                    pe.wait_ge(b_loaded, 16 * g)
                    pe.wait_ge(g_out_ready, g)
                    for j in range(J):
                        last = PE.transpose(group_turned[:, j, :], nat_b[:, j * P:(j + 1) * P], ident[:])
                    last.then_inc(b_turned, 1)

                def turn_a(g):
                    pe.wait_ge(a_ordered, g)
                    pe.wait_ge(b_low, g)
                    for k in range(J):
                        last = PE.transpose(group_turned[:, k, :], by_k[:, k * P:(k + 1) * P], ident[:])
                    last.then_inc(a_turned, 1)

                def join(g):
                    pe.wait_ge(a_low, g)
                    for j in range(J):
                        for k, (a, b) in enumerate(((0, 0), (0, 1), (1, 0))):
                            last = PE.matmul(group_g, a1c[:, a, j, :], m.bt[:, bass.ds(g * 8, 8), b, j, :],
                                             start=(j == 0 and k == 0), stop=(j == J - 1 and k == 2))
                    last.then_inc(g_done, 1)

                def body(i, first=False, last=False, group=False, next_group=False):
                    for u in range(U):
                        if not (last and u == 3):
                            turn(i, u + 1)
                        convolve(i, u, first and u < 2)
                        if group and u < 3:
                            (turn_b, turn_a, join)[u](i)

                turns(pe, body)


def pair_stage(nc, m, out):
    ps, ident = m.ps, m.ident
    V, S, PE, GP = nc.vector, nc.scalar, nc.tensor, nc.gpsimd
    TURNS = Q // U
    with ExitStack() as ctx:
        def sem(name):
            return ctx.enter_context(nc.semaphore(name))

        a_gathered = [sem(f"a_gathered{u}") for u in range(U)]
        out_stored = [sem(f"out_stored{u}") for u in range(2)]
        cleared = sem("cleared")
        a_idx = sem("a_idx")
        held_gather = sem("held_gather")
        b_selected = sem("b_selected")
        m_selected = sem("m_selected")
        turned_done, z_done, qt_done, mq_done, o_done = (sem(n) for n in ("turned_done", "z_done", "qt_done", "mq_done", "o_done"))
        x1Th_ready, x1Tl_ready = sem("x1Th_ready"), sem("x1Tl_ready")
        x1h_ready, x1l_ready = sem("x1h_ready"), sem("x1l_ready")
        zh_ready, zl_ready, qt_ready, qh_ready, ql_ready = (sem(n) for n in ("zh_ready", "zl_ready", "qt_ready", "qh_ready", "ql_ready"))
        out_ready = sem("out_ready")

        psT = ps[:, 0:2, :].rearrange("p s (j n) -> p (s j) n", n=P)
        psZ = ps[:, 6, 0:64]
        psQ = ps[0:64, 7, 0:P]
        psM = ps[:, 7, P:2 * P]
        out_dst = out.rearrange("b c t -> (b c) t")

        def turns(eng, body):
            body(0, True, False)
            with eng.Fori(1, TURNS - 1) as i:
                body(i, False, False)
            body(TURNS - 1, False, True)

        with nc.Block() as block:
            @block.sync
            def _(sp):
                def store(p, u):
                    sp.wait_ge(out_ready, p + 1)
                    sp.dma_start(out_dst[bass.ds(p * P, P), :], m.outt[:, u % 2, :]).then_inc(out_stored[u % 2], 16)

                def body(i, first, last):
                    for u in range(U):
                        p = i * U + u
                        if not (last and u):
                            if not (first and u == 0):
                                sp.wait_ge(x1l_ready, p)
                            load_x1(m, sp, p + 3, (u + 3) % U)
                        if not (first and u < 2):
                            store(p - 2, u)

                turns(sp, body)
                store(Q - 2, 0)
                store(Q - 1, 1)
                for u in range(2):
                    sp.wait_ge(out_stored[u], 16 * (Q // 2))

            @block.gpsimd
            def _(gp):
                GP.memset(m.qt[:], 0.0).then_inc(cleared, 1)
                GP.memset(m.mp[:], 0.0).then_inc(cleared, 1)
                gp.wait_ge(cleared, 2)
                for slot in range(2):
                    for copy in range(2):
                        for b in range(2):
                            GP.tensor_copy(m.mp[32 * b:32 * b + 32, slot, copy, 32 * b:32 * b + R],
                                           ident[32 * b:32 * b + 32, 32 * b:32 * b + R]).then_inc(cleared, 1)
                gp.wait_ge(cleared, 10)

                def body(i, first, last):
                    for u in range(U):
                        p = i * U + u
                        if not first:
                            gp.wait_ge(o_done, p - U + 1)
                        GP.tensor_copy(m.idx_now[:, u, 0:1], m.idx_a[:, bass.ds(p, 1)]).then_inc(a_idx, 1)
                        gp.wait_ge(a_idx, p + 1)
                        gp.sem_inc(held_gather, 1)
                        gp.indirect_dma_start(m.asel[:, u, :], None, m.a_rows,
                                              bass.IndirectOffsetOnAxis(ap=m.idx_now[:, u, 0:1], axis=0)).then_inc(a_gathered[u], 16)
                        if not (first and u < 2):
                            gp.wait_ge(mq_done, p - 1)
                        for copy in range(2):
                            GP.tensor_copy(m.mp[:, u % 2, copy, :].rearrange("p (b l r) -> p b l r", b=2, l=2)[:, :, 1, :],
                                           m.g_pairs[:, bass.ds(p, 1), :, :].rearrange("p o b r -> p (o b) r")).then_inc(m_selected, 1)

                turns(gp, body)

            @block.scalar
            def _(act):
                def high_turned(p, u):
                    act.wait_ge(turned_done, p + 1)
                    if u >= 2:
                        act.wait_ge(z_done, p - 1)
                    S.activation(m.xTh[:, u % 2, :, :], psT, ACT.Copy).then_inc(x1Th_ready, 1)

                def high(p, u, count):
                    act.wait_ge(m.x1_loaded[u % U], count)
                    S.activation(m.x1h[:, u % U, :], m.xt[:, u % U, :], ACT.Copy).then_inc(x1h_ready, 1)

                def body(i, first, last):
                    for u in range(U):
                        p = i * U + u
                        if not (first and u < 2):
                            act.wait_ge(o_done, p - 1)
                            if not (first and u < 4):
                                act.wait_ge(out_stored[u % 2], 16 * (2 * i + u // 2 - 1))
                            S.activation(m.outt[:, u % 2, :], ps[:, 2 + 2 * (u % 2):4 + 2 * (u % 2), :].rearrange("p s n -> p (s n)"),
                                         ACT.Identity, bias=m.bias_t[:, bass.ds(p - 2, 1)]).then_inc(out_ready, 1)
                        if not (first and u == 0):
                            high_q(p - 1, u - 1)
                        if not (last and u == 3):
                            high_turned(p + 1, (u + 1 if first else 2 + (u + 1) % 2))
                            high(p + 1, u + 1, 16 * (i + 1 + (u + 1) // U))

                def high_q(p, u):
                    act.wait_ge(mq_done, p + 1)
                    S.activation(m.qh[:, u % 2, :], psM, ACT.Copy).then_inc(qh_ready, 1)

                high_turned(0, 0)
                high(0, 0, 16)
                turns(act, body)
                high_q(Q - 1, 1)
                for u in range(2):
                    act.wait_ge(o_done, Q - 1 + u)
                    act.wait_ge(out_stored[u], 16 * (Q // 2 - 1))
                    S.activation(m.outt[:, u, :], ps[:, 2 + 2 * u:4 + 2 * u, :].rearrange("p s n -> p (s n)"),
                                 ACT.Identity, bias=m.bias_t[:, Q - 2 + u:Q - 1 + u]).then_inc(out_ready, 1)

            @block.vector
            def _(dve):
                def low_turned(p, u):
                    dve.wait_ge(x1Th_ready, p + 1)
                    V.tensor_tensor(m.xTl[:, u % 2, :, :], psT, m.xTh[:, u % 2, :, :], ALU.subtract).then_inc(x1Tl_ready, 1)

                def load_ids(p, pairs):
                    _, ids = nc.values_load_multi_w_load_instructions(
                        m.sel_ids[:].rearrange("o q b l -> o (q b l)")[:, bass.ds(4 * p, 4 * pairs)],
                        engines=(mybir.EngineType.DVE,), min_val=0, max_val=N2 - 1,
                        skip_runtime_bounds_check_because="an adapter's number is below the count of its table's adapters")
                    return ids

                def select(ids, u):
                    for n in range(4):
                        table = m.bt[:, N1:, :, :, :] if n % 2 else m.bt[:, 0:N2, :, :, :]
                        V.tensor_copy(m.bsel[:, u % 2, n, :, :, :].rearrange("p s j r -> p (s j r)"),
                                      table[:, bass.ds(ids[n], 1), :, :, :].rearrange("p o s j r -> p (o s j r)")).then_inc(b_selected, 1)

                def body(i, first, last):
                    for u in range(U):
                        p = i * U + u
                        dve.wait_ge(z_done, p + 1)
                        V.tensor_scalar(m.zh[:], psZ, 1 / A_SCALE, None, ALU.mult).then_inc(zh_ready, 1)
                        dve.wait_ge(zh_ready, p + 1)
                        V.scalar_tensor_tensor(m.zl[:], psZ, 1 / A_SCALE, m.zh[:], ALU.mult, ALU.subtract).then_inc(zl_ready, 1)
                        if not (last and u == 3):
                            low_turned(p + 1, u + 1)
                        if u == 0:
                            ids = load_ids(p + 2, 2 if last else U)
                        if not (last and u >= 2):
                            select(ids[4 * u:4 * u + 4], u)
                        dve.wait_ge(qt_done, p + 1)
                        for b in range(2):
                            rows, part = slice(32 * b, 32 * b + 32), slice(64 * b, 64 * b + 64)
                            V.tensor_copy(m.qt[rows, part], psQ[rows, part]).then_inc(qt_ready, 1)
                        dve.wait_ge(x1h_ready, p + 1)
                        V.tensor_tensor(m.x1l[:, u, :], m.xt[:, u, :], m.x1h[:, u, :], ALU.subtract).then_inc(x1l_ready, 1)
                        dve.wait_ge(qh_ready, p + 1)
                        V.tensor_tensor(m.ql[:, u % 2, :], psM[0:64, :], m.qh[0:64, u % 2, :], ALU.subtract).then_inc(ql_ready, 1)
                dve.wait_ge(cleared, 10)
                ids = load_ids(0, 2)
                for p in range(2):
                    select(ids[4 * p:4 * p + 4], p)
                low_turned(0, 0)
                turns(dve, body)

            @block.tensor
            def _(pe):
                def turn(p, u, count):
                    pe.wait_ge(m.x1_loaded[u % U], count)
                    for j in range(J):
                        last = PE.transpose(psT[:, j, :], m.xt[:, u % U, j * P:(j + 1) * P], ident[:])
                    last.then_inc(turned_done, 1)

                def mix(p, u, bank, early):
                    if bank == 0:
                        pe.wait_ge(x1l_ready, p + 1)
                        if not early:
                            pe.wait_ge(out_ready, p - 1)
                    o = ps[:, 2 + 2 * (u % 2) + bank, :]
                    cut = slice(bank * 512, bank * 512 + 512)
                    for k, (w, xp) in enumerate(((m.iwh, m.x1h), (m.iwh, m.x1l), (m.iwl, m.x1h))):
                        PE.matmul(o, w[:, bass.ds(p, 1), :].rearrange("p o d -> p (o d)"), xp[:, u, cut], start=(k == 0), stop=False)

                def turn_q(p, u):
                    pe.wait_ge(qt_ready, 2 * p + 2)
                    pe.wait_ge(m_selected, 2 * p + 2)
                    PE.matmul(psM, m.mp[:, u % 2, :, :].rearrange("p c n -> p (c n)"), m.qt[:], start=True, stop=True).then_inc(mq_done, 1)

                def add_adapters(p, u, count):
                    pe.wait_ge(ql_ready, p + 1)
                    pe.wait_ge(a_gathered[u], count)
                    for bank in range(2):
                        o = ps[:, 2 + 2 * (u % 2) + bank, :]
                        cut = slice(bank * 512, bank * 512 + 512)
                        PE.matmul(o, m.qh[:, u % 2, :], m.asel[:, u, cut], start=False, stop=False)
                        last = PE.matmul(o, m.ql[:, u % 2, :], m.asel[0:64, u, cut], start=False, stop=True)
                    last.then_inc(o_done, 1)

                def body(i, first, last):
                    for u in range(U):
                        p = i * U + u
                        has_prev = not (first and u == 0)
                        pu = (u - 1) % U
                        pe.wait_ge(x1Tl_ready, p + 1)
                        if not (last and u == 3):
                            turn(p + 1, u + 1, 16 * (i + 1 + (u + 1) // U))
                        if has_prev:
                            turn_q(p - 1, pu)
                        pe.wait_ge(b_selected, 4 * p + 4)
                        for j in range(J):
                            for k, (xT, b) in enumerate(((m.xTh, 0), (m.xTh, 1), (m.xTl, 0))):
                                done = PE.matmul(psZ, xT[:, u % 2, j, :], m.bsel[:, u % 2, :, b, j, :],
                                                 start=(j == 0 and k == 0), stop=(j == J - 1 and k == 2))
                        done.then_inc(z_done, 1)
                        if has_prev:
                            mix(p - 1, pu, 0, first and u < 3)
                            mix(p - 1, pu, 1, False)
                        pe.wait_ge(zl_ready, p + 1)
                        if has_prev:
                            pe.wait_ge(ql_ready, p)
                        for k, (z, w) in enumerate(((m.zh, m.iwh), (m.zh, m.iwl), (m.zl, m.iwh))):
                            done = PE.matmul(psQ, z[:], w[:, bass.ds(p, 1), :].rearrange("p o d -> p (o d)"), start=(k == 0), stop=(k == 2))
                        done.then_inc(qt_done, 1)
                        if has_prev:
                            add_adapters(p - 1, pu, 16 * (i + 1) if u else 16 * i)

                turn(0, 0, 16)
                turns(pe, body)
                turn_q(Q - 1, 3)
                mix(Q - 1, 3, 0, False)
                mix(Q - 1, 3, 1, False)
                add_adapters(Q - 1, 3, 16 * TURNS)


def program(nc, x, lens, id1, id2, id3, log_dt, C, log_A_real, A_imag, D, A1, B1, A2, B2, W, bias, out):
    with ExitStack() as ctx:
        m = storage(nc, ctx)
        setup_stage(nc, m, x, lens, id1, id2, id3, log_dt, C, log_A_real, A_imag, D, A1, B1, bias)
        channel_stage(nc, m, x, W, A2, B2)
        pair_stage(nc, m, out)


_INS = ['x', 'itok_B_8_3872', 'itok_B_3_7', 'itok_B_4_50', 'itok_B_0_31', 'L0_cond_log_dt', 'L0_cond_C', 'L0_cond_log_A_real',
        'L0_cond_A_imag', 'L0_cond_D', 'L1_cond_A', 'L1_cond_B', 'L2_cond_A', 'L2_cond_B', 'L3_cond_weights', 'L3_cond_biases']


def kernel(**inputs):
    import numpy as _np
    import concourse.bacc as _bacc
    from concourse import mybir as _mybir
    from concourse.bass_utils import run_bass_kernel_spmd as _run

    nc = _bacc.Bacc("TRN2", target_bir_lowering=False, num_devices=1)
    arrays, args = {}, []
    for name in _INS:
        a = _np.ascontiguousarray(inputs[name])
        arrays[f"in_{name}"] = a
        args.append(nc.dram_tensor(f"in_{name}", a.shape, _mybir.dt.from_np(a.dtype), kind="ExternalInput").ap())
    args.append(nc.dram_tensor("out_dram", inputs["x"].shape, F32, kind="ExternalOutput").ap())
    program(nc, *args)
    r = _run(nc, [arrays], core_ids=[0])
    return r.results[0]["out_dram"]
```
